# Optimizing a Trainium2 kernel written in Bass

```python
import numpy as np
import jax
import jax.numpy as jnp

def _softmax(x, axis=-1):
    return jax.nn.softmax(x, axis=axis)

def _gelu(x):
    return jax.nn.gelu(x, approximate=True)

def _silu(x):
    return jax.nn.silu(x)

def _sigmoid(x):
    return jax.nn.sigmoid(x)

def _layernorm(x, axis=-1, eps=1e-05):
    m = jnp.mean(x, axis=axis, keepdims=True)
    v = jnp.var(x, axis=axis, keepdims=True)
    return (x - m) / jnp.sqrt(v + eps)

def _scatter_add(tgt, idx, src, axis=0):
    return tgt.at[idx].add(src)

def _segment_sum(src, seg, n):
    return jax.ops.segment_sum(src, seg, n)
kernel_name = 'mk_adaln_d1_jaxref_r4_84484e'

def setup_inputs(seed: int=0):
    np.random.seed(seed)
    _w = jnp.asarray

    def _L0_attn_setup():
        import jax, jax.numpy as jnp
        import numpy as np
        NUM_HEADS = 16
        ROPE_BASE = 10000.0

        def _rotate_half(x):
            half = x.shape[-1] // 2
            x1, x2 = (x[..., :half], x[..., half:])
            return jnp.concatenate((-x2, x1), axis=-1)

        def _rope_cos_sin(seq_len, dim, dtype):
            inv_freq = 1.0 / ROPE_BASE ** (jnp.arange(0, dim, 2, dtype=jnp.float32) / dim)
            t = jnp.arange(seq_len, dtype=jnp.float32)
            freqs = jnp.einsum('i,j->ij', t, inv_freq)
            emb = jnp.concatenate((freqs, freqs), axis=-1)
            return (emb.astype(dtype), None)
        key = jax.random.key(seed)
        k1, k2, k3 = jax.random.split(key, 3)
        B, S, D = (4, 256, 512)
        return {'hidden_states': jax.random.normal(k1, (B, S, D), dtype=jnp.float32), 'w_qkv': jax.random.normal(k2, (3 * D, D), dtype=jnp.float32) * 0.02, 'b_qkv': jax.random.normal(k3, (3 * D,), dtype=jnp.float32) * 0.02}
    _L0_attn_in = _L0_attn_setup()

    def _L0_ffn_setup():
        import jax, jax.numpy as jnp
        import numpy as np
        TOP_K = 4

        def _silu_and_mul(gu):
            g, u = jnp.split(gu, 2, axis=-1)
            return jax.nn.silu(g) * u
        key = jax.random.key(seed)
        ks = jax.random.split(key, 7)
        H, E, I, Is = (512, 16, 352, 1408)
        s = 0.02
        return {'hidden_states': jax.random.normal(ks[0], (4, 256, H), dtype=jnp.float32), 'gate_w': jax.random.normal(ks[1], (E, H), dtype=jnp.float32) * s, 'sgate_w': jax.random.normal(ks[2], (1, H), dtype=jnp.float32) * s, 'w13': jax.random.normal(ks[3], (E, 2 * I, H), dtype=jnp.float32) * s, 'w2': jax.random.normal(ks[4], (E, H, I), dtype=jnp.float32) * s, 'shared_gate_up_w': jax.random.normal(ks[5], (2 * Is, H), dtype=jnp.float32) * s, 'shared_down_w': jax.random.normal(ks[6], (H, Is), dtype=jnp.float32) * s}
    _L0_ffn_in = _L0_ffn_setup()
    _L0_c = _w((lambda *s: np.random.randn(*s).astype(np.float32) * 0.05)(1, 512))
    _L0_wmod = _w((lambda *s: np.random.randn(*s).astype(np.float32) * 0.05)(512, 6 * 512) * 512 ** (-0.5))
    _d = {'L0_attn_hidden_states': _L0_attn_in['hidden_states'], 'L0_attn_w_qkv': _L0_attn_in['w_qkv'], 'L0_attn_b_qkv': _L0_attn_in['b_qkv'], 'L0_ffn_gate_w': _L0_ffn_in['gate_w'], 'L0_ffn_sgate_w': _L0_ffn_in['sgate_w'], 'L0_ffn_w13': _L0_ffn_in['w13'], 'L0_ffn_w2': _L0_ffn_in['w2'], 'L0_ffn_shared_gate_up_w': _L0_ffn_in['shared_gate_up_w'], 'L0_ffn_shared_down_w': _L0_ffn_in['shared_down_w'], 'L0_c': _L0_c, 'L0_wmod': _L0_wmod}
    _x0 = _d['L0_attn_hidden_states']
    _d['L0_attn_hidden_states'] = jax.random.normal(jax.random.fold_in(jax.random.key(seed), 1), (1, 2048, 512), dtype=_x0.dtype)
    del _x0
    return _d

def reference(L0_attn_hidden_states, L0_attn_w_qkv, L0_attn_b_qkv, L0_ffn_gate_w, L0_ffn_sgate_w, L0_ffn_w13, L0_ffn_w2, L0_ffn_shared_gate_up_w, L0_ffn_shared_down_w, L0_c, L0_wmod):

    def _L0_attn_ref(hidden_states, w_qkv, b_qkv):
        import jax, jax.numpy as jnp
        import numpy as np
        NUM_HEADS = 16
        ROPE_BASE = 10000.0

        def _rotate_half(x):
            half = x.shape[-1] // 2
            x1, x2 = (x[..., :half], x[..., half:])
            return jnp.concatenate((-x2, x1), axis=-1)

        def _rope_cos_sin(seq_len, dim, dtype):
            inv_freq = 1.0 / ROPE_BASE ** (jnp.arange(0, dim, 2, dtype=jnp.float32) / dim)
            t = jnp.arange(seq_len, dtype=jnp.float32)
            freqs = jnp.einsum('i,j->ij', t, inv_freq)
            emb = jnp.concatenate((freqs, freqs), axis=-1)
            return (emb.astype(dtype), None)
        B, S, D = hidden_states.shape
        H = NUM_HEADS
        hd = D // H
        qkv = jnp.einsum('bsd,ed->bse', hidden_states, w_qkv) + b_qkv
        qkv = qkv.reshape(B, S, H, 3 * hd)
        q = jnp.transpose(qkv[..., :hd], (0, 2, 1, 3))
        k = jnp.transpose(qkv[..., hd:2 * hd], (0, 2, 1, 3))
        v = jnp.transpose(qkv[..., 2 * hd:], (0, 2, 1, 3))
        emb, _ = _rope_cos_sin(S, hd, hidden_states.dtype)
        cos = jnp.cos(emb)[None, None, :, :]
        sin = jnp.sin(emb)[None, None, :, :]
        q = q * cos + _rotate_half(q) * sin
        k = k * cos + _rotate_half(k) * sin
        norm = jnp.sqrt(jnp.asarray(hd, dtype=jnp.float32)).astype(q.dtype)
        scores = jnp.einsum('bhqd,bhkd->bhqk', q, k) / norm
        causal = jnp.tril(jnp.ones((S, S), dtype=bool))[None, None]
        mask_value = jnp.finfo(scores.dtype).min
        scores = jnp.where(causal, scores, mask_value)
        attn = jax.nn.softmax(scores, axis=-1)
        out = jnp.einsum('bhqk,bhkd->bhqd', attn, v)
        return jnp.transpose(out, (0, 2, 1, 3)).reshape(B, S, D)

    def _L0_ffn_ref(hidden_states, gate_w, sgate_w, w13, w2, shared_gate_up_w, shared_down_w):
        import jax, jax.numpy as jnp
        import numpy as np
        TOP_K = 4

        def _silu_and_mul(gu):
            g, u = jnp.split(gu, 2, axis=-1)
            return jax.nn.silu(g) * u
        B, S, H = hidden_states.shape
        x = hidden_states.reshape(-1, H)
        E = gate_w.shape[0]
        shared = _silu_and_mul(x @ shared_gate_up_w.T) @ shared_down_w.T
        shared = shared * jax.nn.sigmoid(x @ sgate_w.T)
        router_logits = x @ gate_w.T
        routing_weights = jax.nn.softmax(router_logits.astype(jnp.float32), axis=-1)
        topk_w, topk_ids = jax.lax.top_k(routing_weights, TOP_K)

        def body(acc, ew):
            w13_e, w2_e, e = ew
            coef = jnp.sum(jnp.where(topk_ids == e, topk_w, 0.0), axis=-1)
            h = _silu_and_mul(x @ w13_e.T)
            acc = acc + (h @ w2_e.T).astype(jnp.float32) * coef[:, None]
            return (acc, None)
        init = jnp.zeros((x.shape[0], H), dtype=jnp.float32)
        sparse_out, _ = jax.lax.scan(body, init, (w13, w2, jnp.arange(E)))
        out = shared + sparse_out.astype(x.dtype)
        return out.reshape(B, S, H)
    x = L0_attn_hidden_states
    mod = (_silu(L0_c) @ L0_wmod).reshape(L0_c.shape[0], 6, 1, -1)
    sa, ca, ga, sb, cb, gb = (mod[:, 0], mod[:, 1], mod[:, 2], mod[:, 3], mod[:, 4], mod[:, 5])
    ga = (2 * (ga >= 0) - 1) * jnp.maximum(jnp.abs(ga), 0.25)
    gb = (2 * (gb >= 0) - 1) * jnp.maximum(jnp.abs(gb), 0.25)
    h = _layernorm(x, axis=-1) * (1 + ca) + sa
    x = x + ga * _L0_attn_ref(h, L0_attn_w_qkv, L0_attn_b_qkv)
    h = _layernorm(x, axis=-1) * (1 + cb) + sb
    x = x + gb * _L0_ffn_ref(h, L0_ffn_gate_w, L0_ffn_sgate_w, L0_ffn_w13, L0_ffn_w2, L0_ffn_shared_gate_up_w, L0_ffn_shared_down_w)
    return x

_drawn_inputs = setup_inputs


def setup_inputs(seed=0):
    import zlib

    import numpy as np

    out = dict(_drawn_inputs(seed))
    spreads = {}
    factors = {'L0_attn_w_qkv': 7.533,
     'L0_attn_b_qkv': 8.0,
     'L0_ffn_gate_w': 8.0,
     'L0_ffn_sgate_w': 8.0,
     'L0_ffn_w13': 8.0,
     'L0_ffn_w2': 8.0,
     'L0_ffn_shared_gate_up_w': 5.439,
     'L0_ffn_shared_down_w': 5.43,
     'L0_c': 3.981,
     'L0_wmod': 3.985}
    for name, (base, spread) in spreads.items():
        noise = np.random.default_rng([zlib.crc32(name.encode()), seed]).standard_normal(out[name].shape)
        drawn = base * np.exp(spread * noise) if base else spread * noise
        out[name] = jnp.asarray(drawn.astype(out[name].dtype))
    for name, factor in factors.items():
        out[name] = (out[name] * factor).astype(out[name].dtype)
    return out
```

```python
import numpy as np
import concourse.bass as bass
from concourse import mybir
from concourse.alu_op_type import AluOpType as ALU
from contextlib import ExitStack

F32 = mybir.dt.float32
F32R = mybir.dt.float32r
BF16 = mybir.dt.bfloat16
I32 = mybir.dt.int32
U32 = mybir.dt.uint32
ACT = mybir.ActivationFunctionType
X = mybir.AxisListType.X

P = 128
TOKENS = 2048
DIM = 512
HEADS = 16
HEAD = DIM // HEADS
KC = DIM // P
TT = TOKENS // P
EXPERTS = 16
TOP = 4
INNER = 352
SHARED = 1408
EPS = 1e-5
MASKED = -1e30


def staged(eng, n, stages, period=2, peeled=0):
    leads = [lead for _, lead in stages]
    start, end = peeled - min(leads), n - max(leads)
    end -= (end - start) % period

    def step(s):
        for stage, lead in stages:
            if 0 <= s + lead < n:
                stage(s + lead, (s + lead) % period)

    for s in range(-max(leads), start):
        step(s)
    with eng.Fori(0, (end - start) // period) as i:
        for u in range(period):
            for stage, lead in stages:
                stage(period * i + (start + u + lead), (start + u + lead) % period)
    for s in range(end, n - min(leads)):
        step(s)


def settle(eng, settled):
    eng.sem_inc(settled, 1)


def tile_of(ap, t):
    if isinstance(t, int):
        return ap[:, t]
    return ap[:, bass.ds(t, 1)].squeeze(1)


def rows_of(dram, t, rows=P):
    return dram[bass.ds(t * rows, rows), :]


def norm_and_project(nc, persist, x, w_qkv_t, b_qkv, rope, c, w_mod_t):
    ctx = ExitStack()
    with ctx:
        def sb(name, shape, dt=F32):
            return ctx.enter_context(nc.sbuf_tensor(name, shape, dt))

        def sem(name):
            return ctx.enter_context(nc.semaphore(name))

        E3 = 3 * DIM
        w_hi = persist.wide_hi[:, :, 0:E3]
        w_lo = persist.wide_lo[:, :, 0:E3]
        bias = sb("bias", [P, E3])
        rope_sb = sb("rope_sb", [P, TT, 2, HEAD])
        cvec = sb("cvec", [P, 4, KC])
        c_rows = sb("c_rows", [P, KC, P])
        x_sb = sb("x_sb", [P, 2, DIM])
        stats = sb("stats", [P, 6])
        mv = sb("mv", [P, 2])
        small = sb("small", [P, 4])
        h = sb("h", [P, 2, DIM])
        hT_hi = persist.wide_hi[:, 0:2, E3:E3 + DIM]
        hT_lo = persist.wide_lo[:, 0:2, E3:E3 + DIM]
        qk = sb("qk", [P, 2, 2 * DIM])
        qk_cos = sb("qk_cos", [P, 2, 2 * DIM])
        qk_sin = sb("qk_sin", [P, 2 * DIM])
        ps_t = [ctx.enter_context(nc.psum_tensor(f"ps_t{i}", [P, DIM], F32)) for i in range(2)]
        ps_qkv = [ctx.enter_context(nc.psum_tensor(f"ps_qkv{i}", [P, E3], F32)) for i in range(2)]
        first_mod = sb("first_mod", [P, 2, DIM])
        later = qk[:].rearrange("p u (j n) -> p (u j) n", n=DIM)
        mod = [first_mod[:, 0], first_mod[:, 1], later[:, 0], later[:, 1], later[:, 2], later[:, 3]]
        ident = persist.ident
        R, V = persist.R, persist.V
        sgn, mag = qk_sin[:, 0:DIM], qk_sin[:, DIM:2 * DIM]
        flat_R = R[:].rearrange("p t n -> p (t n)")
        flat_V = V[:].rearrange("p t g f -> p (t g f)")
        w_raw = [flat_R[:, 8 * 2 * DIM + k * E3:8 * 2 * DIM + (k + 1) * E3] for k in range(KC)]
        w_mod = [flat_R[:, j * KC * DIM:(j + 1) * KC * DIM] for j in range(4)]
        w_mod += [flat_V[:, j * KC * DIM:(j + 1) * KC * DIM] for j in range(2)]

        c_loaded = sem("c_loaded")
        tables_loaded = sem("tables_loaded")
        wmod_loaded = [sem(f"wmod_loaded{i}") for i in range(6)]
        w_loaded = [sem(f"w_loaded{i}") for i in range(KC)]
        x_loaded = [sem(f"x_loaded{i}") for i in range(2)]
        c_exp = sem("c_exp")
        c_ready = sem("c_ready")
        mod_summed = sem("mod_summed")
        mod_ready = sem("mod_ready")
        w_hi_ready = sem("w_hi_ready")
        w_lo_ready = sem("w_lo_ready")
        var_ready = sem("var_ready")
        std_ready = sem("std_ready")
        xn_ready = sem("xn_ready")
        h_ready = sem("h_ready")
        hT_summed = sem("hT_summed")
        hT_hi_ready = sem("hT_hi_ready")
        hT_lo_ready = sem("hT_lo_ready")
        qkv_summed = sem("qkv_summed")
        qk_ready = sem("qk_ready")
        qkv_read = sem("qkv_read")
        cos_ready = sem("cos_ready")
        rotated = sem("rotated")
        vec_step = sem("vec_step")
        pool_step = sem("pool_step")
        h_scaled = sem("h_scaled")
        ident_step = sem("ident_step")
        gate_step = sem("gate_step")
        gates_ready = sem("gates_ready")
        mod_kept = sem("mod_kept")
        ident_ready = sem("ident_ready")

        block = ctx.enter_context(nc.Block())

        @block.sync
        def _(sync):
            sync.dma_start(cvec[:, 0, :], c).then_inc(c_loaded, 16)
            def load_mod(j):
                sync.dma_start(w_mod[j], w_mod_t[:, j].rearrange("p k n -> p (k n)")).then_inc(wmod_loaded[j], 16)

            load_mod(0)
            load_mod(1)
            sync.dma_start(x_sb[:, 0], x[0:P, :]).then_inc(x_loaded[0], 16)
            for k in range(KC):
                sync.dma_start(w_raw[k], w_qkv_t[:, k]).then_inc(w_loaded[k], 16)
            sync.dma_start(bias[:], b_qkv.partition_broadcast(P)).then_inc(tables_loaded, 16)
            sync.dma_start(rope_sb[:], rope).then_inc(tables_loaded, 16)
            for j in range(2, 6):
                load_mod(j)
            sync.dma_start(x_sb[:, 1], x[P:2 * P, :]).then_inc(x_loaded[1], 16)

            def load_x(t, u):
                sync.wait_ge(xn_ready, t - 1)
                sync.dma_start(x_sb[:, u], rows_of(x, t)).then_inc(x_loaded[u], 16)

            load_x(2, 0)
            load_x(3, 1)
            sync.wait_ge(gates_ready, 2)
            sync.wait_ge(mod_ready, 6)
            sync.dma_start(persist.mod_dram, later).then_inc(mod_kept, 16)
            with sync.Fori(1, TT // 2 - 1) as i:
                for u in (0, 1):
                    load_x(2 * i + u + 2, u)

        @block.gpsimd
        def _(pool):
            nc.gpsimd.memset(ident[:], 0.0).then_inc(ident_step, 1)
            pool.wait_ge(ident_step, 1)
            nc.gpsimd.affine_select(out=ident[:], in_=ident[:], compare_op=ALU.not_equal, fill=1.0, base=0,
                                    pattern=[[-1, P]], channel_multiplier=1).then_inc(ident_ready, 1)
            pool.wait_ge(mod_ready, 2)
            pool.wait_ge(tables_loaded, 32)

            def modulate(t, u):
                pool.wait_ge(xn_ready, t + 1)
                nc.gpsimd.tensor_tensor(h[:, u], h[:, u], mod[1], ALU.mult).then_inc(h_scaled, 1)
                pool.wait_ge(h_scaled, t + 1)
                nc.gpsimd.tensor_tensor(h[:, u], h[:, u], mod[0], ALU.add).then_inc(h_ready, 1)

            def times_cos(t, u):
                pool.wait_ge(qk_ready, t + 1)
                settle(pool, persist.settled)
                cos = tile_of(rope_sb[:, :, 0], t).unsqueeze(1).to_broadcast([P, 2 * HEADS, HEAD])
                nc.gpsimd.tensor_tensor(qk_cos[:, u].rearrange("p (g f) -> p g f", f=HEAD),
                                        qk[:, u].rearrange("p (g f) -> p g f", f=HEAD), cos,
                                        ALU.mult).then_inc(cos_ready, 1)

            staged(pool, TT, [(modulate, 2), (times_cos, -1)])

        @block.scalar
        def _(act):
            act.wait_ge(c_loaded, 16)
            nc.scalar.activation(cvec[:, 1], cvec[:, 0], ACT.Exp, scale=-1.0).then_inc(c_exp, 1)

            def evacuate_mod(j):
                act.wait_ge(mod_summed, j + 1)
                nc.scalar.activation(mod[j], ps_t[j % 2][:], ACT.Copy,
                                     bias=1.0 if j in (1, 4) else 0.0).then_inc(mod_ready, 1)

            for k in range(KC):
                if k < 2:
                    evacuate_mod(k)
                act.wait_ge(w_loaded[k], 16)
                nc.scalar.activation(w_hi[:, k], w_raw[k], ACT.Copy).then_inc(w_hi_ready, 1)
            for j in range(2, 6):
                evacuate_mod(j)

            def std(t, u):
                act.wait_ge(var_ready, t + 1)
                nc.scalar.activation(small[:, 1:2], small[:, 0:1], ACT.Sqrt).then_inc(std_ready, 1)

            def split_hi(t, u):
                act.wait_ge(hT_summed, t + 1)
                nc.scalar.activation(hT_hi[:, u], ps_t[u][:], ACT.Copy).then_inc(hT_hi_ready, 1)

            staged(act, TT, [(std, 2), (split_hi, 1)])

        @block.vector
        def _(vec):
            vec.wait_ge(c_exp, 1)
            nc.vector.tensor_scalar(cvec[:, 2], cvec[:, 1], 1.0, None, ALU.add).then_inc(vec_step, 1)
            vec.wait_ge(vec_step, 1)
            nc.vector.reciprocal(cvec[:, 2], cvec[:, 2]).then_inc(vec_step, 1)
            vec.wait_ge(vec_step, 2)
            nc.vector.tensor_tensor(cvec[:, 3], cvec[:, 2], cvec[:, 0], ALU.mult).then_inc(vec_step, 1)
            vec.wait_ge(vec_step, 3)
            nc.vector.tensor_copy(c_rows[:], cvec[:, 3].unsqueeze(2).to_broadcast([P, KC, P])).then_inc(c_ready, 1)
            for k in range(KC):
                vec.wait_ge(w_hi_ready, k + 1)
                nc.vector.tensor_tensor(w_lo[:, k], w_raw[k], w_hi[:, k].bitcast(F32),
                                        ALU.subtract).then_inc(w_lo_ready, 1)

            base = 3
            NORM_STEPS = 3

            def normalise(t, u):
                s = base + t * NORM_STEPS
                vec.wait_ge(x_loaded[u], 16 * ((t - u) // 2 + 1) if isinstance(t, int) else (t - u) * 8 + 16)
                nc.vector.bn_stats(stats[:], x_sb[:, u]).then_inc(vec_step, 1)
                vec.wait_ge(vec_step, s + 1)
                settle(vec, persist.settled)
                nc.vector.bn_aggr(mv[:], stats[:]).then_inc(vec_step, 1)
                vec.wait_ge(vec_step, s + 2)
                nc.vector.tensor_scalar(small[:, 0:1], mv[:, 1:2], EPS, None, ALU.add).then_inc(var_ready, 1)
                vec.wait_ge(std_ready, t + 1)
                nc.vector.reciprocal(small[:, 2:3], small[:, 1:2]).then_inc(vec_step, 1)
                vec.wait_ge(vec_step, s + 3)
                nc.vector.tensor_scalar(h[:, u], x_sb[:, u], mv[:, 0:1], small[:, 2:3],
                                        ALU.subtract, ALU.mult).then_inc(xn_ready, 1)

            def split_lo(t, u):
                vec.wait_ge(hT_hi_ready, t + 1)
                nc.vector.tensor_tensor(hT_lo[:, u], ps_t[u][:], hT_hi[:, u].bitcast(F32),
                                        ALU.subtract).then_inc(hT_lo_ready, 1)

            def gates():
                for n, j in enumerate((2, 5)):
                    vec.wait_ge(mod_ready, j + 1)
                    nc.vector.tensor_scalar(sgn, mod[j], 0.0, 2.0, ALU.is_ge, ALU.mult).then_inc(gate_step, 1)
                    nc.vector.scalar_tensor_tensor(mag, mod[j], -1.0, mod[j], ALU.mult, ALU.max).then_inc(gate_step, 1)
                    vec.wait_ge(gate_step, 3 * n + 2)
                    nc.vector.tensor_scalar(mag, mag, 0.25, None, ALU.max).then_inc(gate_step, 1)
                    vec.wait_ge(gate_step, 3 * n + 3)
                    nc.vector.scalar_tensor_tensor(mod[j], sgn, -1.0, mag, ALU.add, ALU.mult).then_inc(gates_ready, 1)
                    vec.wait_ge(gates_ready, n + 1)
                vec.wait_ge(mod_kept, 16)

            def add_bias(t, u):
                if isinstance(t, int) and t == 0:
                    gates()
                vec.wait_ge(qkv_summed, t + 1)
                nc.vector.tensor_tensor(qk[:, u], ps_qkv[u][:, 0:2 * DIM], bias[:, 0:2 * DIM],
                                        ALU.add).then_inc(qk_ready, 1)
                nc.vector.tensor_tensor(tile_of(V, t)[:, :, 0:HEAD],
                                        ps_qkv[u][:, 2 * DIM:].rearrange("p (g f) -> p g f", f=HEAD),
                                        bias[:, 2 * DIM:].rearrange("p (g f) -> p g f", f=HEAD),
                                        ALU.add).then_inc(qkv_read, 1)

            def rotate(t, u):
                half = HEAD // 2
                vec.wait_ge(qk_ready, t + 1)
                src = qk[:, u].rearrange("p (g f) -> p g f", f=HEAD)
                dst = qk_sin[:].rearrange("p (g f) -> p g f", f=HEAD)
                sin = tile_of(rope_sb[:, :, 1], t)
                vec.wait_ge(rotated, 2 * t)
                nc.vector.tensor_tensor(dst[:, :, 0:half], src[:, :, half:],
                                        sin[:, 0:half].unsqueeze(1).to_broadcast([P, 2 * HEADS, half]), ALU.mult)
                nc.vector.tensor_tensor(dst[:, :, half:], src[:, :, 0:half],
                                        sin[:, half:].unsqueeze(1).to_broadcast([P, 2 * HEADS, half]),
                                        ALU.mult).then_inc(rotated, 1)
                vec.wait_ge(rotated, 2 * t + 1)
                vec.wait_ge(cos_ready, t + 1)
                nc.vector.tensor_tensor(tile_of(R, t), qk_cos[:, u], qk_sin[:], ALU.add).then_inc(rotated, 1)

            vec.wait_ge(tables_loaded, 32)
            staged(vec, TT, [(normalise, 2), (split_lo, 1), (add_bias, -1), (rotate, -2)])
            nc.vector.memset(V[:, :, :, HEAD:HEAD + 1], 1.0)
        @block.tensor
        def _(pe):
            pe.wait_ge(c_ready, 1)

            def modulation(j):
                pe.wait_ge(wmod_loaded[j], 16)
                if j >= 2:
                    pe.wait_ge(mod_ready, j - 1)
                for k in range(KC):
                    last = nc.tensor.matmul(ps_t[j % 2][:], c_rows[:, k], w_mod[j][:, k * DIM:(k + 1) * DIM],
                                            start=k == 0, stop=k == KC - 1)
                last.then_inc(mod_summed, 1)

            for j in range(6):
                modulation(j)
            pe.wait_ge(ident_ready, 1)
            pe.wait_ge(mod_ready, 6)

            def transpose_h(t, u):
                pe.wait_ge(h_ready, t + 1)
                for k in range(KC):
                    last = nc.tensor.transpose(ps_t[u][:, k * P:(k + 1) * P], h[:, u, k * P:(k + 1) * P], ident[:])
                last.then_inc(hT_summed, 1)

            def project(t, u):
                pe.wait_ge(hT_lo_ready, t + 1)
                pe.wait_ge(qkv_read, t + 1)
                for n in range(3):
                    for k in range(KC):
                        ks = slice(k * P, (k + 1) * P)
                        ns = slice(n * DIM, (n + 1) * DIM)
                        for m, (a, b) in enumerate(((hT_lo, w_hi), (hT_hi, w_lo), (hT_hi, w_hi))):
                            last = nc.tensor.matmul(ps_qkv[u][:, ns], a[:, u, ks], b[:, k, ns],
                                                    start=k == 0 and m == 0, stop=k == KC - 1 and m == 2)
                last.then_inc(qkv_summed, 1)

            pe.wait_ge(w_lo_ready, KC)
            pe.sem_inc(qkv_read, 2)
            staged(pe, TT, [(transpose_h, 1), (project, 0)])



PAIRS = HEADS // 2
AHEAD = 1.08
SLICE = 4
STACK = 3 * HEAD


def prepare_events():
    GROUPS = TT // SLICE
    groups = [(hh, g) for hh in range(2) for g in range(GROUPS)]
    turn = [[("T", dict(hh=hh, kind=kind, g=g)) for kind in range(2)] for hh, g in groups] + [[]]
    events, m = list(turn[0]), 0
    for (hh, g), coming in zip(groups, turn[1:]):
        scores = []
        for qt in range(SLICE * g, SLICE * g + SLICE):
            end = (qt + 1) * P
            for n, start in enumerate(range(0, end, DIM)):
                stop = min(start + DIM, end)
                wide = start if stop - start >= 2 * P or start == 0 else start - P
                scores.append(("M", dict(hh=hh, g=g, qt=qt, n=n, start=start, stop=stop, wide=wide, m=m)))
                m += 1
        if hh == 1 and g == 0:
            places = ((4, coming[1]), (2, ("N", dict(hh=0))), (1, coming[0]))
        else:
            places = tuple(zip((len(scores) // 2 + 1, 1), reversed(coming)))
        for place, event in places:
            scores.insert(place, event)
        events += scores
        if g == GROUPS - 1:
            events.append(("R", dict(hh=hh, seen=m)))
    return events + [("N", dict(hh=1))], m


def attend_events(first=False, last=False):
    events, b, blocks = [], 0, []
    for s in range(TT // SLICE):
        for kt in range(SLICE * (s + 1)):
            blocks.append(dict(b=b, s=s, kt=kt, skip=max(0, kt - SLICE * s) * P, last=kt == SLICE * (s + 1) - 1))
            b += 1
    late = {} if first else {2: dict(s=TT // SLICE - 1, carried=True)}
    for n in range(len(blocks) + 1):
        if n < len(blocks):
            events.append(("S", blocks[n]))
        if n in late:
            events.append(("O", late[n]))
        if n:
            events.append(("A", blocks[n - 1]))
            if blocks[n - 1]["last"]:
                events.append(("E", dict(s=blocks[n - 1]["s"], blocks=n)))
                late[n + 2] = dict(s=blocks[n - 1]["s"])
    if last:
        events += [("O", e) for n, e in late.items() if n > len(blocks)]
    return events, b


def merged(prepare, attend):
    def cost(kind, e):
        return max(e["stop"] - e["wide"], P) / DIM + 0.1 if kind == "M" else {"T": 0.4, "N": 0.4, "R": 1.2}[kind]

    def share(kind, e):
        return {"S": 0.35, "A": 0.65}.get(kind, 0.0) * (1 - e["skip"] / DIM / 2) if kind in "SA" else 0.0

    total, work = sum(cost(k, e) for k, e in prepare), sum(share(k, e) for k, e in attend)
    out, left, spent, done = [], list(prepare), 0.0, 0.0
    for kind, e in attend:
        out.append((kind, e))
        done += share(kind, e) / work
        while left and spent < total * min(1.0, done * AHEAD):
            spent += cost(*left[0])
            out.append(left.pop(0))
    return out + left


def numbered(events):
    out, use, turned = [], 0, {}
    for kind, e in events:
        out.append((kind, dict(e, use=use, turned=turned.get((e["hh"], e["g"])) if kind == "M" else 0)))
        use += kind in "TNO"
        if kind == "T":
            turned[e["hh"], e["g"]] = use
    return out, use


def attention(nc, persist):
    prepare, M_UNITS = prepare_events()
    first, BLOCKS = attend_events(first=True)
    first, _ = numbered(merged(prepare, first))
    both, STEP_USES = numbered(merged(prepare, attend_events()[0]))
    last, _ = numbered(attend_events(last=True)[0])
    prepare, FIRST_USES = numbered(prepare)
    SLICES = TT // SLICE
    CREDITS = 2
    ctx = ExitStack()
    with ctx:
        def sb(name, shape, dt=F32):
            return ctx.enter_context(nc.sbuf_tensor(name, shape, dt))

        def psum(name, shape):
            return ctx.enter_context(nc.psum_tensor(name, shape, F32))

        def sem(name):
            return ctx.enter_context(nc.semaphore(name))

        R, V, ident = persist.R, persist.V, persist.ident
        qT = [[persist.wide_hi[:, 2 * i + j] for j in range(2)] for i in range(2)]
        kT = [[persist.wide_lo[:, 2 * i + j] for j in range(2)] for i in range(2)]
        stack = [[sb(f"{name}_stack{hh}", [P, TT, STACK], F32R) for name in "kq"] for hh in range(2)]
        v_pair = [sb(f"v_pair{i}", [P, TT, 2, HEAD + 1]) for i in range(2)]
        probs = [sb(f"probs{i}", [P, 2, DIM]) for i in range(2)]
        part_max = sb("part_max", [P, TT, SLICE])
        row_max = sb("row_max", [P, TT])
        neg_max = sb("neg_max", [P, 2, TT], F32R)
        own_tile = sb("own_tile", [32, TT], BF16)
        ident_bf = sb("ident_bf", [P, P], BF16)
        mask = sb("mask", [P, P], BF16)
        o_sb = sb("o_sb", [HEAD + 1, 2, DIM])
        o_inv = sb("o_inv", [P, SLICE, 2, 1])
        ps_s = [psum(f"ps_s{i}", [P, 2, DIM]) for i in range(2)]
        ps_m = [psum(f"ps_m{i}", [P, DIM]) for i in range(2)]
        ps_o = psum("ps_o", [P, DIM])
        ps_x = psum("ps_x", [P, DIM])

        const_step = sem("const_step")
        const_ready = sem("const_ready")
        rows_set = sem("rows_set")
        stack_ready = sem("stack_ready")
        v_ready = sem("v_ready")
        x_ready = sem("x_ready")
        x_taken = sem("x_taken")
        m_ready = sem("m_ready")
        m_taken = sem("m_taken")
        max_step = sem("max_step")
        neg_ready = sem("neg_ready")
        s_ready = sem("s_ready")
        p_ready = sem("p_ready")
        p_used = sem("p_used")
        o_taken = sem("o_taken")
        inv_ready = sem("inv_ready")
        block = ctx.enter_context(nc.Block())

        def walk(handle):
            def run(eng):
                def step(p, u, events):
                    for kind, e in events:
                        ahead = FIRST_USES + e["use"] if events is first else p * STEP_USES + (FIRST_USES - 1 + e["use"])
                        if kind in "TMRN":
                            handle(eng, kind, p + 1, 1 - u, e, ahead)
                        elif "carried" in e:
                            handle(eng, kind, p - 1, 1 - u, e, ahead)
                        else:
                            handle(eng, kind, p, u, e, ahead)

                for kind, e in prepare:
                    handle(eng, kind, 0, 0, e, e["use"])
                step(0, 0, first)
                with eng.Fori(0, PAIRS // 2 - 2) as i:
                    for u in (1, 0):
                        step(2 * i + (2 - u), u, both)
                step(PAIRS - 3, 1, both)
                step(PAIRS - 2, 0, both)
                step(PAIRS - 1, 1, last)
            return run

        @block.gpsimd
        def _(pool):
            nc.gpsimd.memset(own_tile[:], 0.0).then_inc(const_step, 1)
            nc.gpsimd.memset(ident_bf[:], 0.0).then_inc(const_step, 1)
            nc.gpsimd.memset(mask[:], 0.0).then_inc(const_step, 1)

            BUILD = 6

            def build(q, hh):
                done = (q * 2 + hh) * BUILD
                for kind, (parts, low) in enumerate((((0, 1), 2), ((0, 2), 1))):
                    col = (1 - kind) * DIM + q * (2 * HEAD) + hh * HEAD
                    src = R[:, :, bass.ds(col, HEAD)]
                    dst = [stack[hh][kind][:, :, n * HEAD:(n + 1) * HEAD] for n in range(3)]
                    for n in parts:
                        nc.gpsimd.tensor_copy(dst[n], src).then_inc(stack_ready, 1)
                    pool.wait_ge(stack_ready, done + 3 * kind + 2)
                    settle(pool, persist.settled)
                    nc.gpsimd.tensor_tensor(dst[low], src, dst[0].bitcast(F32), ALU.subtract).then_inc(stack_ready, 1)

            pool.wait_ge(const_step, 3)
            build(0, 0)
            build(0, 1)
            nc.gpsimd.affine_select(out=ident_bf[:], in_=ident_bf[:], compare_op=ALU.not_equal, fill=1.0, base=0,
                                    pattern=[[-1, P]], channel_multiplier=1).then_inc(const_ready, 1)
            nc.gpsimd.affine_select(out=mask[:], in_=mask[:], compare_op=ALU.is_ge, fill=MASKED, base=0,
                                    pattern=[[-1, P]], channel_multiplier=1).then_inc(const_ready, 1)
            for part in range(2):
                nc.gpsimd.affine_select(out=own_tile[:], in_=own_tile[:], compare_op=ALU.not_equal, fill=1.0,
                                        base=-TT * part, pattern=[[-1, TT]],
                                        channel_multiplier=1).then_inc(const_ready, 1)
                pool.wait_ge(const_ready, 3 + part)

            def handle(eng, kind, q, u, e, ahead):
                if kind == "T" and e["g"] == TT // SLICE - 1 and e["kind"] == 1:
                    eng.wait_ge(x_ready, ahead + 1)
                    if e["hh"] == 0:
                        nc.gpsimd.tensor_copy(v_pair[u][:], V[:, :, bass.ds(q * 2, 2), :]).then_inc(v_ready, 1)
                    if not isinstance(q, int) or q < PAIRS - 1:
                        build(q + 1, e["hh"])

            walk(handle)(pool)

        @block.scalar
        def _(act):
            def handle(eng, kind, q, u, e, ahead):
                if kind == "T":
                    g = e["g"]
                    dst = (kT, qT)[e["kind"]][u][e["hh"]][0:STACK, g * DIM:(g + 1) * DIM]
                    eng.wait_ge(x_ready, ahead + 1)
                    nc.scalar.activation(dst, ps_x[0:STACK, :], ACT.Copy).then_inc(x_taken, 1)
                elif kind == "S":
                    b, n = e["b"] % 2, q * BLOCKS + e["b"]
                    eng.wait_ge(s_ready, n + 1)
                    eng.wait_ge(p_used, n + 1)
                    nc.scalar.activation(probs[b][:, :, e["skip"]:], ps_s[b][:, :, e["skip"]:], ACT.Exp,
                                         scale=HEAD ** -0.5).then_inc(p_ready, 1)
                elif kind == "E":
                    eng.wait_ge(p_used, q * BLOCKS + (e["blocks"] + CREDITS))
                    eng.wait_ge(x_ready, ahead)
                    nc.scalar.activation(o_sb[:, 0], ps_o[0:HEAD + 1, :], ACT.Copy).then_inc(o_taken, 1)

            walk(handle)(act)

        @block.vector
        def _(vec):
            for i in range(2):
                for j in range(2):
                    nc.vector.memset(kT[i][j][STACK:P, :].bitcast(F32), 1.0).then_inc(rows_set, 1)
            nc.vector.memset(part_max[:], -3e38).then_inc(rows_set, 1)
            vec.wait_ge(rows_set, 5)
            vec.wait_ge(const_ready, 4)

            def handle(eng, kind, q, u, e, ahead):
                if kind == "M":
                    m = q * M_UNITS + e["m"]
                    eng.wait_ge(m_ready, m + 1)
                    nc.vector.reduce_max(part_max[:, e["qt"], e["n"]:e["n"] + 1],
                                         ps_m[e["m"] % 2][:, e["start"] - e["wide"]:e["stop"] - e["wide"]],
                                         X).then_inc(m_taken, 1)
                elif kind == "R":
                    head = q * 2 + e["hh"]
                    eng.wait_ge(m_taken, q * M_UNITS + (e["seen"] + CREDITS))
                    nc.vector.reduce_max(row_max[:], part_max[:], X).then_inc(max_step, 1)
                    eng.wait_ge(max_step, head * 2 + 1)
                    nc.vector.tensor_scalar(neg_max[:, 0], row_max[:], -1.0, None, ALU.mult).then_inc(max_step, 1)
                    eng.wait_ge(max_step, head * 2 + 2)
                    nc.vector.scalar_tensor_tensor(neg_max[:, 1], row_max[:], -1.0, neg_max[:, 0].bitcast(F32),
                                                   ALU.mult, ALU.subtract).then_inc(neg_ready, 1)
                elif kind == "N":
                    eng.wait_ge(x_ready, ahead + 1)
                    nc.vector.tensor_tensor(qT[u][e["hh"]][STACK:P, :].rearrange("p (t n) -> p t n", n=P),
                                            ps_x[0:32, 0:P].unsqueeze(1).to_broadcast([32, TT, P]),
                                            own_tile[:].unsqueeze(2).to_broadcast([32, TT, P]),
                                            ALU.mult).then_inc(x_taken, 1)
                elif kind == "E":
                    eng.wait_ge(p_used, q * BLOCKS + (e["blocks"] + CREDITS))
                    eng.wait_ge(x_ready, ahead)
                    nc.vector.tensor_copy(o_sb[:, 1], ps_o[64:64 + HEAD + 1, :]).then_inc(o_taken, 1)
                elif kind == "O":
                    s = e["s"]
                    eng.wait_ge(x_ready, ahead + 1)
                    o = ps_x[:, 0:SLICE * 2 * (HEAD + 1)].rearrange("p (j h f) -> p j h f", h=2, f=HEAD + 1)
                    nc.vector.reciprocal(o_inv[:], o[:, :, :, HEAD:]).then_inc(inv_ready, 1)
                    eng.wait_ge(inv_ready, q * SLICES + (s + 1))
                    dst = R[:, SLICE * s:SLICE * (s + 1), bass.ds(q * (2 * HEAD), 2 * HEAD)]
                    nc.vector.tensor_tensor(dst.rearrange("p j (h f) -> p j h f", h=2), o[:, :, :, 0:HEAD],
                                            o_inv[:].to_broadcast([P, SLICE, 2, HEAD]), ALU.mult).then_inc(x_taken, 1)

            walk(handle)(vec)

        @block.tensor
        def _(pe):
            pe.sem_inc(m_taken, CREDITS)
            pe.sem_inc(p_ready, CREDITS)
            pe.sem_inc(p_used, CREDITS)
            pe.wait_ge(const_ready, 4)
            pe.wait_ge(rows_set, 5)

            def handle(eng, kind, q, u, e, ahead):
                if kind in "TNO":
                    eng.wait_ge(x_taken, ahead)
                if kind == "T":
                    if e["g"] == 0 and e["kind"] == 0:
                        eng.wait_ge(stack_ready, (q * 2 + (e["hh"] + 1)) * 6)
                    for j in range(SLICE):
                        last = nc.tensor.transpose(ps_x[0:STACK, j * P:(j + 1) * P],
                                                   stack[e["hh"]][e["kind"]][:, SLICE * e["g"] + j, :].bitcast(F32), ident[:])
                    last.then_inc(x_ready, 1)
                elif kind == "M":
                    m, start, stop = q * M_UNITS + e["m"], e["wide"], e["stop"]
                    qs = slice(e["qt"] * P, (e["qt"] + 1) * P)
                    bank = ps_m[e["m"] % 2]
                    diagonal = stop == (e["qt"] + 1) * P
                    eng.wait_ge(x_taken, ahead - e["use"] + e["turned"])
                    eng.wait_ge(m_taken, m + 1)
                    last = nc.tensor.matmul(bank[:, 0:stop - start], qT[u][e["hh"]][0:STACK, qs],
                                            kT[u][e["hh"]][0:STACK, start:stop], start=True, stop=not diagonal)
                    if diagonal:
                        last = nc.tensor.matmul(bank[:, stop - start - P:stop - start], ident_bf[:], mask[:],
                                                start=False, stop=True)
                    last.then_inc(m_ready, 1)
                elif kind == "N":
                    eng.wait_ge(neg_ready, q * 2 + (e["hh"] + 1))
                    nc.tensor.transpose(ps_x[0:32, 0:P], neg_max[:].rearrange("p a t -> p (a t)").bitcast(F32),
                                        ident[:]).then_inc(x_ready, 1)
                elif kind == "S":
                    b, n, skip = e["b"] % 2, q * BLOCKS + e["b"], e["skip"]
                    if e["b"] == 0:
                        eng.wait_ge(x_taken, ahead)
                        eng.wait_ge(v_ready, q + 1)
                    eng.wait_ge(p_ready, n + 1)
                    qs = slice(e["s"] * DIM + skip, (e["s"] + 1) * DIM)
                    diagonal = e["kt"] >= SLICE * e["s"]
                    for hh in range(2):
                        last = nc.tensor.matmul(ps_s[b][:, hh, skip:], kT[u][hh][:, e["kt"] * P:(e["kt"] + 1) * P],
                                                qT[u][hh][:, qs], start=True, stop=not diagonal)
                        if diagonal:
                            last = nc.tensor.matmul(ps_s[b][:, hh, skip:skip + P], mask[:], ident_bf[:],
                                                    start=False, stop=True)
                    last.then_inc(s_ready, 1)
                elif kind == "A":
                    b, n, skip = e["b"] % 2, q * BLOCKS + e["b"], e["skip"]
                    eng.wait_ge(p_ready, n + (1 + CREDITS))
                    if e["kt"] == 0:
                        eng.wait_ge(o_taken, (q * SLICES + e["s"]) * 2)
                    for hh in range(2):
                        last = nc.tensor.matmul(ps_o[64 * hh:64 * hh + HEAD + 1, skip:], v_pair[u][:, e["kt"], hh, :],
                                                probs[b][:, hh, skip:], start=e["kt"] == 0, stop=e["last"])
                    last.then_inc(p_used, 1)
                elif kind == "O":
                    eng.wait_ge(o_taken, (q * SLICES + (e["s"] + 1)) * 2)
                    settle(eng, persist.settled)
                    for j in range(SLICE):
                        for hh in range(2):
                            at = (j * 2 + hh) * (HEAD + 1)
                            last = nc.tensor.transpose(ps_x[:, at:at + HEAD + 1], o_sb[:, hh, j * P:(j + 1) * P],
                                                       ident[0:HEAD + 1, 0:HEAD + 1])
                    last.then_inc(x_ready, 1)

            walk(handle)(pe)



SLOTS = 2 * P
SLOT_TILES = (TOKENS * TOP - EXPERTS) // SLOTS + EXPERTS
MOST = TOKENS // SLOTS
LOGITS = EXPERTS + 1


def norm_and_route(nc, persist, x, gates_t):
    ctx = ExitStack()
    with ctx:
        def sb(name, shape, dt=F32):
            return ctx.enter_context(nc.sbuf_tensor(name, shape, dt))

        def sem(name):
            return ctx.enter_context(nc.semaphore(name))

        R, ident = persist.R, persist.ident
        h2T_hi, h2T_lo = persist.wide_hi, persist.wide_lo
        mod = sb("mod2", [P, 3, DIM])
        gate_raw = sb("gate_raw", [P, KC, LOGITS])
        gate_hi = sb("gate_hi", [P, KC, LOGITS], F32R)
        gate_lo = sb("gate_lo", [P, KC, LOGITS], F32R)
        x_in = sb("x_in", [P, 2, DIM])
        x1 = sb("x1", [P, 2, DIM])
        h2 = sb("h2", [P, 2, DIM])
        stats = sb("stats2", [P, 6])
        mv = sb("mv2", [P, 2])
        small = sb("small2", [P, 4])
        logitsT = sb("logitsT", [LOGITS, TOKENS])
        logits = sb("logits", [P, TT, LOGITS])
        top_logit = sb("top_logit", [P, TT, 1])
        shifted = sb("shifted", [P, TT, EXPERTS])
        exps = sb("exps", [P, TT, EXPERTS])
        exp_sum = sb("exp_sum", [P, TT, 1])
        exp_inv = sb("exp_inv", [P, TT, 1])
        routing = sb("routing", [P, TT, EXPERTS])
        gate_exp = sb("gate_exp", [P, TT])
        top_index = sb("top_index", [P, TT, 8], U32)
        top_number = sb("top_number", [P, TT, TOP])
        chosen = sb("chosen", [P, TT, TOP, EXPERTS])
        picked = sb("picked", [P, TT, TOP, EXPERTS])
        member = sb("member", [P, TT, EXPERTS], BF16)
        counts = sb("counts", [P, EXPERTS, 1])
        above = sb("above", [P, EXPERTS, MOST])
        n_tiles = sb("n_tiles", [P, 1, EXPERTS])
        earlier = sb("earlier", [P, EXPERTS, EXPERTS])
        first_tile = sb("first_tile", [P, EXPERTS])
        end_tile = sb("end_tile", [P, 1, EXPERTS])
        first_slot = sb("first_slot", [P, 1, EXPERTS])
        slot_of = sb("slot_of", [P, TT, EXPERTS])
        slot_number = sb("slot_number", [P, TT, TOP])
        passed = sb("passed", [P, SLOT_TILES, EXPERTS])
        tile_number = sb("tile_number", [P, SLOT_TILES])
        expert_iota = sb("expert_iota", [P, EXPERTS])
        full_iota = sb("full_iota", [P, 1, MOST])
        tile_iota = sb("tile_iota", [P, SLOT_TILES, 1])
        before = sb("before", [P, EXPERTS, EXPERTS])
        earlier_tok = sb("earlier_tok", [P, P], BF16)
        ones_bf = sb("ones_bf", [P, P], BF16)
        token_id = sb("token_id", [P, TT], I32)
        put_slot = sb("put_slot", [P, 2, TOP], I32)
        put_token = sb("put_token", [P, 2, 1], I32)
        no_token = sb("no_token", [P, SLOT_TILES * 2], I32)
        ps_t = [ctx.enter_context(nc.psum_tensor(f"ps_h{i}", [P, DIM], F32)) for i in range(2)]
        ps_l = [ctx.enter_context(nc.psum_tensor(f"ps_l{i}", [P, DIM], F32)) for i in range(2)]
        ps_g = ctx.enter_context(nc.psum_tensor("ps_g", [P, TT, LOGITS], F32))
        ps_pos = ctx.enter_context(nc.psum_tensor("ps_pos", [P, TT, EXPERTS], F32))
        ps_count = ctx.enter_context(nc.psum_tensor("ps_count", [P, EXPERTS, 1], F32))

        consts_loaded = sem("consts_loaded")
        x_loaded = [sem(f"x_in_loaded{i}") for i in range(2)]
        gate_hi_ready = sem("gate_hi_ready")
        gate_lo_ready = sem("gate_lo_ready")
        scaled = sem("scaled")
        x1_ready = sem("x1_ready")
        x1_stored = [sem(f"x1_stored{i}") for i in range(2)]
        h2_stored = [sem(f"h2_stored{i}") for i in range(2)]
        norm_step = sem("norm_step")
        var_ready = sem("var2_ready")
        std_ready = sem("std2_ready")
        xn_ready = sem("xn2_ready")
        h2_scaled = sem("h2_scaled")
        h2_ready = sem("h2_ready")
        h2T_summed = sem("h2T_summed")
        hi_ready = sem("h2T_hi_ready")
        lo_ready = sem("h2T_lo_ready")
        logitsT_summed = sem("logitsT_summed")
        logitsT_ready = sem("logitsT_ready")
        logits_turned = sem("logits_turned")
        shifted_ready = sem("shifted_ready")
        exps_ready = sem("exps_ready")
        route_step = sem("route_step")
        member_ready = sem("member_ready")
        counted = sem("counted")
        slots_ready = sem("slots_ready")
        const_step = sem("const2_step")
        const_ready = sem("const2_ready")
        put_copied = sem("put_copied")
        cleared = sem("cleared")
        put = [sem(f"put{i}") for i in range(2)]
        block = ctx.enter_context(nc.Block())

        @block.sync
        def _(sync):
            sync.dma_start(mod[:], persist.mod_dram[:, 0:3]).then_inc(consts_loaded, 16)
            sync.dma_start(gate_raw[:], gates_t).then_inc(consts_loaded, 16)
            for u in range(2):
                sync.dma_start(x_in[:, u], rows_of(x, u)).then_inc(x_loaded[u], 16)
            with sync.Fori(0, TT // 2 - 1) as i:
                for u in (0, 1):
                    sync.wait_ge(x1_ready, 2 * i + u + 1)
                    sync.dma_start(rows_of(persist.x1_dram, 2 * i + u), x1[:, u]).then_inc(x1_stored[u], 16)
                    sync.dma_start(x_in[:, u], rows_of(x, 2 * i + u + 2)).then_inc(x_loaded[u], 16)
            for u in range(2):
                sync.wait_ge(x1_ready, TT - 2 + u + 1)
                sync.dma_start(rows_of(persist.x1_dram, TT - 2 + u), x1[:, u]).then_inc(x1_stored[u], 16)
            sync.wait_ge(const_ready, 1)
            for u in range(2):
                sync.wait_ge(x1_stored[u], 16 * (TT // 2))
                sync.wait_ge(h2_stored[u], 16 * (TT // 2))

        @block.gpsimd
        def _(pool):
            nc.gpsimd.memset(no_token[:].bitcast(F32), 0.0).then_inc(const_ready, 1)
            nc.gpsimd.memset(before[:], 1.0).then_inc(const_step, 1)
            nc.gpsimd.memset(earlier_tok[:], 1.0).then_inc(const_step, 1)
            nc.gpsimd.memset(ones_bf[:], 1.0).then_inc(const_ready, 1)
            nc.gpsimd.iota(expert_iota[:], [[1, EXPERTS]], base=0, channel_multiplier=0,
                           allow_small_or_imprecise_dtypes=True).then_inc(const_ready, 1)
            nc.gpsimd.iota(full_iota[:], [[SLOTS, MOST]], base=0, channel_multiplier=0,
                           allow_small_or_imprecise_dtypes=True).then_inc(const_ready, 1)
            nc.gpsimd.iota(tile_iota[:], [[1, SLOT_TILES]], base=0, channel_multiplier=0,
                           allow_small_or_imprecise_dtypes=True).then_inc(const_ready, 1)
            nc.gpsimd.iota(token_id[:], [[P, TT]], base=0, channel_multiplier=1).then_inc(const_ready, 1)
            pool.wait_ge(const_step, 2)
            nc.gpsimd.affine_select(out=before[:], in_=before[:], compare_op=ALU.is_gt, fill=0.0, base=0,
                                    pattern=[[1, EXPERTS], [-1, EXPERTS]], channel_multiplier=0).then_inc(const_ready, 1)
            nc.gpsimd.affine_select(out=earlier_tok[:], in_=earlier_tok[:], compare_op=ALU.is_gt, fill=0.0, base=0,
                                    pattern=[[1, P]], channel_multiplier=-1).then_inc(const_ready, 1)
            pool.wait_ge(const_ready, 8)
            pool.dma_start(persist.slot_token.rearrange("(p c) o -> p (c o)", p=P), no_token[:]).then_inc(cleared, 16)
            pool.wait_ge(consts_loaded, 32)

            def modulate(t, u):
                pool.wait_ge(xn_ready, t + 1)
                nc.gpsimd.tensor_tensor(h2[:, u], h2[:, u], mod[:, 2], ALU.mult).then_inc(h2_scaled, 1)
                pool.wait_ge(h2_scaled, t + 1)
                nc.gpsimd.tensor_tensor(h2[:, u], h2[:, u], mod[:, 1], ALU.add).then_inc(h2_ready, 1)

            staged(pool, TT, [(modulate, 2)])

            pool.wait_ge(cleared, 16)
            pool.wait_ge(slots_ready, 1)

            def enter(t, u):
                done = 16 * TOP * (t // 2) if isinstance(t, int) else (t - u) * (8 * TOP)
                pool.wait_ge(put[u], done)
                nc.gpsimd.tensor_copy(put_slot[:, u], tile_of(persist.slots, t)).then_inc(put_copied, 1)
                nc.gpsimd.tensor_copy(put_token[:, u], token_id[:, t:t + 1] if isinstance(t, int) else
                                      token_id[:, bass.ds(t, 1)]).then_inc(put_copied, 1)
                pool.wait_ge(put_copied, 2 * t + 2)
                settle(pool, persist.settled)
                for j in range(TOP):
                    pool.indirect_dma_start(persist.slot_token,
                                            bass.IndirectOffsetOnAxis(ap=put_slot[:, u, j:j + 1], axis=0),
                                            put_token[:, u], None).then_inc(put[u], 16)

            staged(pool, TT, [(enter, 0)])
            for u in range(2):
                pool.wait_ge(put[u], 16 * TOP * (TT // 2))

        @block.scalar
        def _(act):
            act.wait_ge(consts_loaded, 32)
            nc.scalar.activation(gate_hi[:], gate_raw[:], ACT.Copy).then_inc(gate_hi_ready, 1)

            def std(t, u):
                act.wait_ge(var_ready, t + 1)
                nc.scalar.activation(small[:, 1:2], small[:, 0:1], ACT.Sqrt).then_inc(std_ready, 1)

            def split_hi(t, u):
                act.wait_ge(h2T_summed, t + 1)
                nc.scalar.activation(h2T_hi[:, :, bass.ds(t * P, P)], ps_t[u][:].rearrange("p (k n) -> p k n", n=P),
                                     ACT.Copy).then_inc(hi_ready, 1)

            def store_h2(t, u):
                act.wait_ge(h2_ready, t + 1)
                act.dma_start(rows_of(persist.h2_dram, t), h2[:, u]).then_inc(h2_stored[u], 16)

            staged(act, TT, [(std, 2), (store_h2, 1), (split_hi, 1)])
            for n in range(TOKENS // DIM):
                act.wait_ge(logitsT_summed, n + 1)
                nc.scalar.activation(logitsT[:, n * DIM:(n + 1) * DIM], ps_l[n % 2][0:LOGITS, :],
                                     ACT.Copy).then_inc(logitsT_ready, 1)
            act.wait_ge(shifted_ready, 1)
            nc.scalar.activation(exps[:], shifted[:], ACT.Exp).then_inc(exps_ready, 1)
            nc.scalar.activation(gate_exp[:], logits[:, :, EXPERTS], ACT.Exp, scale=-1.0).then_inc(exps_ready, 1)

        @block.vector
        def _(vec):
            vec.wait_ge(gate_hi_ready, 1)
            nc.vector.tensor_tensor(gate_lo[:], gate_raw[:], gate_hi[:].bitcast(F32), ALU.subtract).then_inc(gate_lo_ready, 1)
            NORM_STEPS = 3

            def residual(t, u):
                vec.wait_ge(x_loaded[u], 16 * (t // 2 + 1) if isinstance(t, int) else (t - u) * 8 + 16)
                vec.wait_ge(x1_stored[u], 16 * (t // 2) if isinstance(t, int) else (t - u) * 8)
                nc.vector.tensor_tensor(x1[:, u], tile_of(R, t)[:, 0:DIM], mod[:, 0], ALU.mult).then_inc(scaled, 1)
                vec.wait_ge(scaled, t + 1)
                nc.vector.tensor_tensor(x1[:, u], x1[:, u], x_in[:, u], ALU.add).then_inc(x1_ready, 1)
                vec.wait_ge(x1_ready, t + 1)

            def normalise(t, u):
                s = t * NORM_STEPS
                nc.vector.bn_stats(stats[:], x1[:, u]).then_inc(norm_step, 1)
                vec.wait_ge(norm_step, s + 1)
                settle(vec, persist.settled)
                nc.vector.bn_aggr(mv[:], stats[:]).then_inc(norm_step, 1)
                vec.wait_ge(norm_step, s + 2)
                nc.vector.tensor_scalar(small[:, 0:1], mv[:, 1:2], EPS, None, ALU.add).then_inc(var_ready, 1)
                vec.wait_ge(std_ready, t + 1)
                nc.vector.reciprocal(small[:, 2:3], small[:, 1:2]).then_inc(norm_step, 1)
                vec.wait_ge(norm_step, s + 3)
                vec.wait_ge(h2_stored[u], 16 * (t // 2) if isinstance(t, int) else (t - u) * 8)
                nc.vector.tensor_scalar(h2[:, u], x1[:, u], mv[:, 0:1], small[:, 2:3],
                                        ALU.subtract, ALU.mult).then_inc(xn_ready, 1)

            def split_lo(t, u):
                vec.wait_ge(hi_ready, t + 1)
                cols = bass.ds(t * P, P)
                nc.vector.tensor_tensor(h2T_lo[:, :, cols], ps_t[u][:].rearrange("p (k n) -> p k n", n=P),
                                        h2T_hi[:, :, cols].bitcast(F32), ALU.subtract).then_inc(lo_ready, 1)

            staged(vec, TT, [(residual, 2), (normalise, 2), (split_lo, 1)])

            steps = [0]

            def then(instruction):
                steps[0] += 1
                instruction.then_inc(route_step, 1)
                vec.wait_ge(route_step, steps[0])

            vec.wait_ge(logits_turned, 1)
            vec.wait_ge(const_ready, 8)
            then(nc.vector.tensor_copy(logits[:], ps_g[:]))
            then(nc.vector.reduce_max(top_logit[:], logits[:, :, 0:EXPERTS], X))
            nc.vector.tensor_tensor(shifted[:], logits[:, :, 0:EXPERTS], top_logit[:].to_broadcast([P, TT, EXPERTS]),
                                    ALU.subtract).then_inc(shifted_ready, 1)
            vec.wait_ge(exps_ready, 2)
            then(nc.vector.tensor_scalar(persist.shared_gate[:], gate_exp[:], 1.0, None, ALU.add))
            then(nc.vector.reciprocal(persist.shared_gate[:], persist.shared_gate[:]))
            then(nc.vector.reduce_sum(exp_sum[:], exps[:], X))
            then(nc.vector.reciprocal(exp_inv[:], exp_sum[:]))
            then(nc.vector.tensor_tensor(routing[:], exps[:], exp_inv[:].to_broadcast([P, TT, EXPERTS]), ALU.mult))
            for t in range(TT):
                last = nc.vector.max(persist.top_weight[:, t], routing[:, t])
            then(last)
            for t in range(TT):
                last = nc.vector.max_index(top_index[:, t], persist.top_weight[:, t], routing[:, t])
            then(last)
            then(nc.vector.tensor_copy(top_number[:], top_index[:, :, 0:TOP]))
            each = [P, TT, TOP, EXPERTS]
            then(nc.vector.tensor_tensor(chosen[:], top_number[:].unsqueeze(3).to_broadcast(each),
                                         expert_iota[:].unsqueeze(1).unsqueeze(1).to_broadcast(each), ALU.is_equal))
            with nc.allow_low_precision(reason="a token picks an expert at most once: 0 or 1"):
                nc.vector.tensor_reduce(member[:], chosen[:].rearrange("p t j e -> p t e j"), axis=X,
                                        op=ALU.add).then_inc(member_ready, 1)
            vec.wait_ge(counted, 1)
            then(nc.vector.tensor_copy(counts[:], ps_count[:]))
            wide = [P, EXPERTS, MOST]
            then(nc.vector.tensor_tensor(above[:], counts[:].to_broadcast(wide), full_iota[:].to_broadcast(wide), ALU.is_gt))
            then(nc.vector.reduce_sum(n_tiles[:, 0], above[:], X))
            then(nc.vector.tensor_tensor(earlier[:], n_tiles[:].to_broadcast([P, EXPERTS, EXPERTS]), before[:], ALU.mult))
            then(nc.vector.reduce_sum(first_tile[:], earlier[:], X))
            then(nc.vector.tensor_tensor(end_tile[:, 0], first_tile[:], n_tiles[:, 0], ALU.add))
            then(nc.vector.tensor_scalar(first_slot[:, 0], first_tile[:], float(SLOTS), None, ALU.mult))
            then(nc.vector.tensor_tensor(slot_of[:], ps_pos[:], first_slot[:].to_broadcast([P, TT, EXPERTS]), ALU.add))
            then(nc.vector.tensor_tensor(picked[:], chosen[:], slot_of[:].unsqueeze(2).to_broadcast(each), ALU.mult))
            then(nc.vector.reduce_sum(slot_number[:], picked[:], X))
            nc.vector.tensor_copy(persist.slots[:], slot_number[:]).then_inc(slots_ready, 1)
            tall = [P, SLOT_TILES, EXPERTS]
            then(nc.vector.tensor_tensor(passed[:], end_tile[:].to_broadcast(tall), tile_iota[:].to_broadcast(tall), ALU.is_le))
            then(nc.vector.reduce_sum(tile_number[:], passed[:], X))
            then(nc.vector.tensor_scalar(tile_number[:], tile_number[:], float(EXPERTS - 1), None, ALU.min))
            then(nc.vector.tensor_copy(persist.tile_expert[:], tile_number[:]))

        @block.tensor
        def _(pe):
            def transpose_h2(t, u):
                pe.wait_ge(h2_ready, t + 1)
                for k in range(KC):
                    last = nc.tensor.transpose(ps_t[u][:, k * P:(k + 1) * P], h2[:, u, k * P:(k + 1) * P], ident[:])
                last.then_inc(h2T_summed, 1)

            staged(pe, TT, [(transpose_h2, 1)])
            pe.wait_ge(lo_ready, TT)
            pe.wait_ge(gate_lo_ready, 1)
            for n in range(TOKENS // DIM):
                if n >= 2:
                    pe.wait_ge(logitsT_ready, n - 1)
                cols = slice(n * DIM, (n + 1) * DIM)
                for k in range(KC):
                    for m, (a, b) in enumerate(((gate_lo, h2T_hi), (gate_hi, h2T_lo), (gate_hi, h2T_hi))):
                        last = nc.tensor.matmul(ps_l[n % 2][0:LOGITS, :], a[:, k, :], b[:, k, cols],
                                                start=k == 0 and m == 0, stop=k == KC - 1 and m == 2)
                last.then_inc(logitsT_summed, 1)
            pe.wait_ge(logitsT_ready, TOKENS // DIM)
            for t in range(TT):
                last = nc.tensor.transpose(ps_g[:, t], logitsT[:, t * P:(t + 1) * P], ident[0:LOGITS, 0:LOGITS])
            last.then_inc(logits_turned, 1)
            pe.wait_ge(member_ready, 1)
            nc.tensor.matmul(ps_pos[:], earlier_tok[:], member[:], start=True, stop=False)
            for t in range(TT - 1):
                nc.tensor.matmul(ps_pos[:, t + 1:], ones_bf[:],
                                 member[:, t].unsqueeze(1).to_broadcast([P, TT - 1 - t, EXPERTS]),
                                 start=False, stop=t == TT - 2)
            for t in range(TT):
                last = nc.tensor.matmul(ps_count[:, :, 0], ones_bf[:], member[:, t], start=t == 0, stop=t == TT - 1)
            last.then_inc(counted, 1)



CHUNKS = SHARED // P
SPANS = TOKENS // DIM


def shared_expert(nc, persist, w_shared_t):
    GU = KC * 2 * P
    ctx = ExitStack()
    with ctx:
        def sb(name, shape, dt=F32):
            return ctx.enter_context(nc.sbuf_tensor(name, shape, dt))

        def sem(name):
            return ctx.enter_context(nc.semaphore(name))

        h2T_hi, h2T_lo, total = persist.wide_hi, persist.wide_lo, persist.shared_sum
        raw = [sb(f"sh_raw{i}", [P, GU + DIM]) for i in range(2)]
        w_hi = [sb(f"sh_hi{i}", [P, GU + DIM], F32R) for i in range(2)]
        w_lo = [sb(f"sh_lo{i}", [P, GU + DIM], F32R) for i in range(2)]
        silu = [sb(f"sh_silu{i}", [P, DIM]) for i in range(2)]
        act_sb = [sb(f"sh_act{i}", [P, DIM]) for i in range(2)]
        a_hi = [sb(f"sh_a_hi{i}", [P, DIM], F32R) for i in range(2)]
        a_lo = [sb(f"sh_a_lo{i}", [P, DIM], F32R) for i in range(2)]
        ps_gu = [ctx.enter_context(nc.psum_tensor(f"ps_gu{i}", [P, 2, DIM], F32)) for i in range(2)]
        ps_y = [ctx.enter_context(nc.psum_tensor(f"ps_y{i}", [P, DIM], F32)) for i in range(4)]

        loaded = [sem(f"sh_loaded{i}") for i in range(2)]
        w_hi_ready = sem("sh_hi_ready")
        w_lo_ready = sem("sh_lo_ready")
        zeroed = sem("sh_zeroed")
        gu_ready = sem("gu_ready")
        silu_ready = sem("silu_ready")
        act_ready = sem("act_ready")
        a_hi_ready = sem("a_hi_ready")
        a_lo_ready = sem("a_lo_ready")
        y_ready = sem("y_ready")
        y_added = sem("y_added")
        block = ctx.enter_context(nc.Block())
        N = CHUNKS * SPANS
        PERIOD = 2 * SPANS

        def chunk_of(t, u):
            return t // SPANS if isinstance(t, int) else (t - u % SPANS) // SPANS

        @block.sync
        def _(sync):
            for j in range(2):
                sync.dma_start(raw[j][:], w_shared_t[j]).then_inc(loaded[j], 16)

            def load(j, u):
                sync.wait_ge(w_hi_ready, j - 1)
                sync.wait_ge(w_lo_ready, j - 1)
                sync.dma_start(raw[u][:], w_shared_t[bass.ds(j, 1)].rearrange("o p n -> p (o n)")).then_inc(loaded[u], 16)

            with sync.Fori(0, (CHUNKS - 2) // 2) as i:
                for u in (0, 1):
                    load(2 * i + 2 + u, u)
            load(CHUNKS - 1, 0)

        @block.scalar
        def _(act):
            def split_weights(j, u):
                act.wait_ge(loaded[u], 16 * (j // 2 + 1) if isinstance(j, int) else (j - u) * 8 + 16)
                nc.scalar.activation(w_hi[u][:], raw[u][:], ACT.Copy).then_inc(w_hi_ready, 1)

            def hidden(t, u):
                v = u % 2
                if u % SPANS == 1 and not (isinstance(t, int) and t > N - SPANS):
                    j = chunk_of(t, u)
                    act.wait_ge(y_ready, (t - u % SPANS) * 4)
                    split_weights(j + 1, (u // SPANS + 1) % 2)
                act.wait_ge(gu_ready, t + 1)
                nc.scalar.activation(silu[v][:], ps_gu[v][:, 0], ACT.Silu).then_inc(silu_ready, 1)
                act.wait_ge(act_ready, t + 1)
                nc.scalar.activation(a_hi[v][:], act_sb[v][:], ACT.Copy).then_inc(a_hi_ready, 1)

            split_weights(0, 0)
            staged(act, N, [(hidden, 0)], PERIOD)

        @block.vector
        def _(vec):
            nc.vector.memset(total[:], 0.0).then_inc(zeroed, 1)
            vec.wait_ge(zeroed, 1)

            def split_weights(j, u):
                vec.wait_ge(w_hi_ready, j + 1)
                nc.vector.tensor_tensor(w_lo[u][:], raw[u][:], w_hi[u][:].bitcast(F32), ALU.subtract).then_inc(w_lo_ready, 1)

            def hidden(t, u):
                v = u % 2
                vec.wait_ge(silu_ready, t + 1)
                nc.vector.tensor_tensor(act_sb[v][:], silu[v][:], ps_gu[v][:, 1], ALU.mult).then_inc(act_ready, 1)
                vec.wait_ge(a_hi_ready, t + 1)
                nc.vector.tensor_tensor(a_lo[v][:], act_sb[v][:], a_hi[v][:].bitcast(F32), ALU.subtract).then_inc(a_lo_ready, 1)
                if u % SPANS == 1 and not (isinstance(t, int) and t > N - SPANS):
                    split_weights(chunk_of(t, u) + 1, (u // SPANS + 1) % 2)

            def add(t, u):
                for c in range(4):
                    vec.wait_ge(y_ready, 4 * t + (c + 1))
                    row = total[:, (u % SPANS) * 4 + c]
                    nc.vector.tensor_tensor(row, row, ps_y[c][:], ALU.add).then_inc(y_added, 1)

            split_weights(0, 0)
            staged(vec, N, [(hidden, 0), (add, -1)], PERIOD)

        @block.tensor
        def _(pe):
            pe.wait_ge(zeroed, 1)
            pe.sem_inc(y_added, 4)

            def up(t, u):
                w, v = (u // SPANS) % 2, u % 2
                if u % SPANS == 0:
                    pe.wait_ge(w_lo_ready, chunk_of(t, u) + 1)
                if not (isinstance(t, int) and t < 2):
                    pe.wait_ge(act_ready, t - 1)
                cols = bass.ds((u % SPANS) * DIM, DIM)
                for half in range(2):
                    for k in range(KC):
                        at = (2 * k + half) * P
                        for m, (a, b) in enumerate(((w_lo, h2T_hi), (w_hi, h2T_lo), (w_hi, h2T_hi))):
                            last = nc.tensor.matmul(ps_gu[v][:, half], a[w][:, at:at + P], b[:, k, cols],
                                                    start=k == 0 and m == 0, stop=k == KC - 1 and m == 2)
                last.then_inc(gu_ready, 1)

            def down(t, u):
                w, v = (u // SPANS) % 2, u % 2
                pe.wait_ge(a_lo_ready, t + 1)
                for c in range(4):
                    rows = slice(c * P, (c + 1) * P)
                    pe.wait_ge(y_added, 4 * t + (c + 1))
                    nc.tensor.matmul(ps_y[c][:], a_lo[v][:, rows], w_hi[w][:, GU:], start=True, stop=False)
                    nc.tensor.matmul(ps_y[c][:], a_hi[v][:, rows], w_lo[w][:, GU:], start=False, stop=False)
                    nc.tensor.matmul(ps_y[c][:], a_hi[v][:, rows], w_hi[w][:, GU:], start=False,
                                     stop=True).then_inc(y_ready, 1)

            staged(pe, N, [(up, 0), (down, -1)], PERIOD)



PARTS = [(0, P), (P, 2 * P), (2 * P, INNER)]
W13 = KC * 2 * INNER
W2 = len(PARTS) * DIM
TAIL = INNER - 2 * P


def routed_experts(nc, persist, w_experts, w_tails):
    ctx = ExitStack()
    with ctx:
        def sb(name, shape, dt=F32):
            return ctx.enter_context(nc.sbuf_tensor(name, shape, dt))

        def sem(name):
            return ctx.enter_context(nc.semaphore(name))

        ident = persist.ident
        raw = [sb(f"ex_raw{i}", [P, W13 + W2]) for i in range(2)]
        flat_hi = persist.wide_hi[:].rearrange("p k n -> p (k n)")
        flat_lo = persist.wide_lo[:].rearrange("p k n -> p (k n)")
        w13_hi = [flat_hi[:, i * W13:(i + 1) * W13] for i in range(2)]
        w13_lo = [flat_lo[:, i * W13:(i + 1) * W13] for i in range(2)]
        w2_hi = [sb(f"w2_hi{i}", [P, W2], F32R) for i in range(2)]
        w2_lo = [sb(f"w2_lo{i}", [P, W2], F32R) for i in range(2)]
        slot_rows = sb("slot_rows", [2 * SLOT_TILES, P], I32)
        slot_rows_f = sb("slot_rows_f", [2 * SLOT_TILES, P])
        slot_tok = sb("slot_tok", [P, 2 * SLOT_TILES], I32)
        now = [sb(f"now{i}", [P, 2], I32) for i in range(2)]
        rows = [sb(f"rows{i}", [P, 2, DIM]) for i in range(2)]
        xT_hi = [sb(f"xT_hi{i}", [P, KC, SLOTS], F32R) for i in range(2)]
        xT_lo = [sb(f"xT_lo{i}", [P, KC, SLOTS], F32R) for i in range(2)]
        silu = sb("ex_silu", [P, 3, SLOTS])
        hidden = sb("ex_hidden", [P, 3, SLOTS])
        a_hi = [sb(f"ex_a_hi{i}", [P, 3, SLOTS], F32R) for i in range(2)]
        a_lo = [sb(f"ex_a_lo{i}", [P, 3, SLOTS], F32R) for i in range(2)]
        y_sb = [sb(f"y_sb{i}", [P, 2, DIM]) for i in range(2)]
        ps_x = ctx.enter_context(nc.psum_tensor("ex_ps_x", [P, KC, SLOTS], F32))
        ps_gu = [ctx.enter_context(nc.psum_tensor(f"ex_ps_gu{i}", [P, 2, SLOTS], F32)) for i in range(3)]
        ps_y = ctx.enter_context(nc.psum_tensor("ex_ps_y", [P, 2, DIM], F32))

        table_loaded = sem("table_loaded")
        table_step = sem("table_step")
        table_turned = sem("table_turned")
        table_ready = sem("table_ready")
        w_loaded = [sem(f"ex_loaded{i}") for i in range(2)]
        now_ready = sem("now_ready")
        gathered = [sem(f"gathered{i}") for i in range(2)]
        x_turned = sem("x_turned")
        x_hi_ready = sem("x_hi_ready")
        x_lo_ready = sem("x_lo_ready")
        w13_hi_ready = sem("w13_hi_ready")
        w13_lo_ready = sem("w13_lo_ready")
        w2_hi_ready = sem("w2_hi_ready")
        w2_lo_ready = sem("w2_lo_ready")
        gu_ready = sem("ex_gu_ready")
        silu_ready = sem("ex_silu_ready")
        hidden_ready = sem("hidden_ready")
        a_hi_ready = sem("ex_a_hi_ready")
        a_lo_ready = sem("ex_a_lo_ready")
        y_ready = sem("ex_y_ready")
        y_taken = sem("y_taken")
        y_stored = [sem(f"y_stored{i}") for i in range(2)]
        block = ctx.enter_context(nc.Block())
        N = SLOT_TILES

        def arrivals(t, u, each=16):
            return each * (t // 2 + 1) if isinstance(t, int) else (t - u) * (each // 2) + each

        @block.sync
        def _(sync):
            sync.dma_start(slot_rows[:], persist.slot_token.rearrange("(c p) o -> c (p o)", p=P)).then_inc(table_loaded, 16)

            def load(t, u):
                if not (isinstance(t, int) and t < 2):
                    sync.wait_ge(w2_hi_ready, 2 * t - 2)
                    sync.wait_ge(w2_lo_ready, 2 * t - 2)
                e = sync.value_load(persist.tile_expert[0:1, t:t + 1] if isinstance(t, int) else
                                    persist.tile_expert[0:1, bass.ds(t, 1)], min_val=0, max_val=EXPERTS - 1)
                sync.dma_start(raw[u][:, 0:W13 + 2 * DIM],
                               w_experts[bass.ds(e, 1)].rearrange("o p n -> p (o n)")).then_inc(w_loaded[u], 16)
                sync.dma_start(raw[u][0:TAIL, W13 + 2 * DIM:],
                               w_tails[bass.ds(e, 1)].rearrange("o p n -> p (o n)")).then_inc(w_loaded[u], 16)

            def store(t, u):
                sync.wait_ge(y_taken, 2 * t + 2)
                to = persist.y_dram[bass.ds(t * SLOTS, SLOTS), :].rearrange("(c p) n -> p c n", p=P)
                sync.dma_start(to, y_sb[u][:]).then_inc(y_stored[u], 16)

            staged(sync, N, [(load, 2), (store, -1)])
            for u in range(2):
                sync.wait_ge(y_stored[u], 16 * ((N + 1 - u) // 2))

        @block.gpsimd
        def _(pool):
            pool.wait_ge(table_ready, 1)

            def gather(t, u):
                if not (isinstance(t, int) and t < 2):
                    pool.wait_ge(x_turned, t - 1)
                nc.gpsimd.tensor_copy(now[u][:], slot_tok[:, 2 * t:2 * t + 2] if isinstance(t, int) else
                                      slot_tok[:, bass.ds(2 * t, 2)]).then_inc(now_ready, 1)
                pool.wait_ge(now_ready, t + 1)
                settle(pool, persist.settled)
                for c in range(2):
                    pool.indirect_dma_start(rows[u][:, c], None, persist.h2_dram,
                                            bass.IndirectOffsetOnAxis(ap=now[u][:, c:c + 1], axis=0)
                                            ).then_inc(gathered[u], 16)

            staged(pool, N, [(gather, 2)], peeled=2)

        @block.scalar
        def _(act):
            def x_hi(t, u):
                act.wait_ge(x_turned, t + 1)
                nc.scalar.activation(xT_hi[u][:], ps_x[:], ACT.Copy).then_inc(x_hi_ready, 1)

            def split_w13(t, u):
                act.wait_ge(w_loaded[u], arrivals(t, u, 32))
                if not (isinstance(t, int) and t < 2):
                    act.wait_ge(gu_ready, 3 * t - 3)
                nc.scalar.activation(w13_hi[u], raw[u][:, 0:W13], ACT.Copy).then_inc(w13_hi_ready, 1)

            def split_w2(t, u):
                if not (isinstance(t, int) and t < 2):
                    act.wait_ge(y_ready, 2 * t - 2)
                nc.scalar.activation(w2_hi[u][:, 0:2 * DIM], raw[u][:, W13:W13 + 2 * DIM],
                                     ACT.Copy).then_inc(w2_hi_ready, 1)
                nc.scalar.activation(w2_hi[u][0:TAIL, 2 * DIM:], raw[u][0:TAIL, W13 + 2 * DIM:],
                                     ACT.Copy).then_inc(w2_hi_ready, 1)

            def activate(t, u):
                for m, (a, b) in enumerate(PARTS):
                    act.wait_ge(gu_ready, 3 * t + (m + 1))
                    nc.scalar.activation(silu[0:b - a, m], ps_gu[m][0:b - a, 0], ACT.Silu).then_inc(silu_ready, 1)
                for m, (a, b) in enumerate(PARTS):
                    act.wait_ge(hidden_ready, 3 * t + (m + 1))
                    nc.scalar.activation(a_hi[u][0:b - a, m], hidden[0:b - a, m], ACT.Copy).then_inc(a_hi_ready, 1)

            def take_y(t, u):
                if not (isinstance(t, int) and t < 2):
                    act.wait_ge(y_stored[u], arrivals(t, u) - 16)
                for c in range(2):
                    act.wait_ge(y_ready, 2 * t + (c + 1))
                    nc.scalar.activation(y_sb[u][:, c], ps_y[:, c], ACT.Copy).then_inc(y_taken, 1)

            staged(act, N, [(x_hi, 1), (split_w13, 1), (activate, 0), (take_y, -1), (split_w2, 1)])

        @block.vector
        def _(vec):
            vec.wait_ge(table_loaded, 16)
            nc.vector.tensor_copy(slot_rows_f[:], slot_rows[:]).then_inc(table_step, 1)
            vec.wait_ge(table_turned, 1)
            nc.vector.tensor_copy(slot_tok[:], ps_x[:].rearrange("p k n -> p (k n)")[:, 0:2 * SLOT_TILES]).then_inc(table_ready, 1)

            def x_lo(t, u):
                vec.wait_ge(x_hi_ready, t + 1)
                nc.vector.tensor_tensor(xT_lo[u][:], ps_x[:], xT_hi[u][:].bitcast(F32), ALU.subtract).then_inc(x_lo_ready, 1)

            def split_w13(t, u):
                vec.wait_ge(w13_hi_ready, t + 1)
                nc.vector.tensor_tensor(w13_lo[u], raw[u][:, 0:W13], w13_hi[u].bitcast(F32),
                                        ALU.subtract).then_inc(w13_lo_ready, 1)

            def split_w2(t, u):
                vec.wait_ge(w2_hi_ready, 2 * t + 2)
                nc.vector.tensor_tensor(w2_lo[u][:, 0:2 * DIM], raw[u][:, W13:W13 + 2 * DIM],
                                        w2_hi[u][:, 0:2 * DIM].bitcast(F32), ALU.subtract).then_inc(w2_lo_ready, 1)
                nc.vector.tensor_tensor(w2_lo[u][0:TAIL, 2 * DIM:], raw[u][0:TAIL, W13 + 2 * DIM:],
                                        w2_hi[u][0:TAIL, 2 * DIM:].bitcast(F32), ALU.subtract).then_inc(w2_lo_ready, 1)

            def multiply(t, u):
                vec.wait_ge(a_lo_ready, 3 * t)
                for m, (a, b) in enumerate(PARTS):
                    vec.wait_ge(silu_ready, 3 * t + (m + 1))
                    nc.vector.tensor_tensor(hidden[0:b - a, m], silu[0:b - a, m], ps_gu[m][0:b - a, 1],
                                            ALU.mult).then_inc(hidden_ready, 1)
                for m, (a, b) in enumerate(PARTS):
                    vec.wait_ge(a_hi_ready, 3 * t + (m + 1))
                    nc.vector.tensor_tensor(a_lo[u][0:b - a, m], hidden[0:b - a, m], a_hi[u][0:b - a, m].bitcast(F32),
                                            ALU.subtract).then_inc(a_lo_ready, 1)

            staged(vec, N, [(x_lo, 1), (split_w13, 1), (multiply, 0), (split_w2, 1)])

        @block.tensor
        def _(pe):
            pe.wait_ge(table_step, 1)
            nc.tensor.transpose(ps_x[:].rearrange("p k n -> p (k n)")[:, 0:2 * SLOT_TILES], slot_rows_f[:],
                                ident[0:2 * SLOT_TILES, 0:2 * SLOT_TILES]).then_inc(table_turned, 1)
            pe.wait_ge(table_ready, 1)

            def turn(t, u):
                pe.wait_ge(gathered[u], arrivals(t, u, 32))
                pe.wait_ge(x_lo_ready, t)
                for c in range(2):
                    for k in range(KC):
                        last = nc.tensor.transpose(ps_x[:, k, c * P:(c + 1) * P], rows[u][:, c, k * P:(k + 1) * P], ident[:])
                last.then_inc(x_turned, 1)

            def up(t, u):
                pe.wait_ge(x_lo_ready, t + 1)
                pe.wait_ge(w13_lo_ready, t + 1)
                for m, (a, b) in enumerate(PARTS):
                    if not (isinstance(t, int) and t == 0):
                        pe.wait_ge(hidden_ready, 3 * t + (m - 2))
                    for half in range(2):
                        for k in range(KC):
                            at = (2 * k + half) * INNER
                            for n, (w, x) in enumerate(((w13_lo, xT_hi), (w13_hi, xT_lo), (w13_hi, xT_hi))):
                                last = nc.tensor.matmul(ps_gu[m][0:b - a, half], w[u][:, at + a:at + b], x[u][:, k],
                                                        start=k == 0 and n == 0, stop=k == KC - 1 and n == 2)
                    last.then_inc(gu_ready, 1)

            def down(t, u):
                pe.wait_ge(a_lo_ready, 3 * t + 3)
                pe.wait_ge(w2_lo_ready, 2 * t + 2)
                for c in range(2):
                    if not (isinstance(t, int) and t == 0):
                        pe.wait_ge(y_taken, 2 * t + (c - 1))
                    for m, (a, b) in enumerate(PARTS):
                        at = slice(m * DIM, (m + 1) * DIM)
                        cols = slice(c * P, (c + 1) * P)
                        for n, (h, w) in enumerate(((a_lo, w2_hi), (a_hi, w2_lo), (a_hi, w2_hi))):
                            last = nc.tensor.matmul(ps_y[:, c], h[u][0:b - a, m, cols], w[u][0:b - a, at],
                                                    start=m == 0 and n == 0, stop=m == 2 and n == 2)
                    last.then_inc(y_ready, 1)

            staged(pe, N, [(turn, 1), (up, 0), (down, -1)], peeled=1)



def combine(nc, persist, out):
    ctx = ExitStack()
    with ctx:
        def sb(name, shape, dt=F32):
            return ctx.enter_context(nc.sbuf_tensor(name, shape, dt))

        def sem(name):
            return ctx.enter_context(nc.semaphore(name))

        gate_b = sb("gate_b", [P, DIM])
        at = [sb(f"at{i}", [P, TOP], I32) for i in range(2)]
        picked = [sb(f"picked_rows{i}", [P, TOP, DIM]) for i in range(2)]
        x1 = [sb(f"x1_in{i}", [P, DIM]) for i in range(2)]
        mixed = [sb(f"mixed{i}", [P, DIM]) for i in range(2)]
        result = [sb(f"result{i}", [P, DIM]) for i in range(2)]
        gate_loaded = sem("gate_b_loaded")
        x1_loaded = [sem(f"x1_loaded{i}") for i in range(2)]
        at_ready = sem("at_ready")
        picked_in = [sem(f"picked_in{i}") for i in range(2)]
        mix_step = sem("mix_step")
        gated = sem("gated")
        result_ready = sem("result_ready")
        stored = [sem(f"stored{i}") for i in range(2)]
        block = ctx.enter_context(nc.Block())
        MIX = 1 + TOP

        def arrivals(t, u, each=16):
            return each * (t // 2 + 1) if isinstance(t, int) else (t - u) * (each // 2) + each

        @block.sync
        def _(sync):
            sync.dma_start(gate_b[:], persist.mod_dram[:, 3]).then_inc(gate_loaded, 16)

            def load(t, u):
                if not (isinstance(t, int) and t < 2):
                    sync.wait_ge(result_ready, t - 1)
                sync.dma_start(x1[u][:], rows_of(persist.x1_dram, t)).then_inc(x1_loaded[u], 16)

            def store(t, u):
                sync.wait_ge(result_ready, t + 1)
                sync.dma_start(rows_of(out, t), result[u][:]).then_inc(stored[u], 16)

            staged(sync, TT, [(load, 1), (store, -1)])
            for u in range(2):
                sync.wait_ge(stored[u], 16 * (TT // 2))

        @block.gpsimd
        def _(pool):
            def gather(t, u):
                if not (isinstance(t, int) and t < 2):
                    pool.wait_ge(mix_step, MIX * t - MIX)
                nc.gpsimd.tensor_copy(at[u][:], tile_of(persist.slots, t)).then_inc(at_ready, 1)
                pool.wait_ge(at_ready, t + 1)
                settle(pool, persist.settled)
                for j in range(TOP):
                    pool.indirect_dma_start(picked[u][:, j], None, persist.y_dram,
                                            bass.IndirectOffsetOnAxis(ap=at[u][:, j:j + 1], axis=0)
                                            ).then_inc(picked_in[u], 16)

            pool.wait_ge(gate_loaded, 16)

            staged(pool, TT, [(gather, 1)], peeled=2)

        @block.vector
        def _(vec):
            vec.wait_ge(gate_loaded, 16)

            def mix(t, u):
                s = t * MIX
                if not (isinstance(t, int) and t < 2):
                    vec.wait_ge(gated, t - 1)
                gate = persist.shared_gate[:, t:t + 1] if isinstance(t, int) else persist.shared_gate[:, bass.ds(t, 1)]
                nc.vector.tensor_scalar(mixed[u][:], tile_of(persist.shared_sum, t), gate, None, ALU.mult).then_inc(mix_step, 1)
                vec.wait_ge(picked_in[u], arrivals(t, u, 16 * TOP))
                for j in range(TOP):
                    vec.wait_ge(mix_step, s + (j + 1))
                    nc.vector.scalar_tensor_tensor(mixed[u][:], picked[u][:, j], tile_of(persist.top_weight, t)[:, j:j + 1],
                                                   mixed[u][:], ALU.mult, ALU.add).then_inc(mix_step, 1)

            def finish(t, u):
                vec.wait_ge(mix_step, MIX * t + MIX)
                if not (isinstance(t, int) and t < 2):
                    vec.wait_ge(stored[u], arrivals(t, u) - 16)
                nc.vector.tensor_tensor(result[u][:], mixed[u][:], gate_b[:], ALU.mult).then_inc(gated, 1)
                vec.wait_ge(gated, t + 1)
                vec.wait_ge(x1_loaded[u], arrivals(t, u))
                nc.vector.tensor_tensor(result[u][:], result[u][:], x1[u][:], ALU.add).then_inc(result_ready, 1)

            staged(vec, TT, [(mix, 0), (finish, -1)])



class Kept:
    pass


def adaln_block(nc, x, w_qkv_t, b_qkv, rope, c, w_mod_t, gates_t, w_shared_t, w_experts, w_tails, out):
    def kept(name, shape, dt=F32):
        return nc.dram_tensor(name, shape, dt, kind="Internal").ap()

    persist = Kept()
    persist.mod_dram = kept("mod_dram", [P, 4, DIM])
    persist.x1_dram = kept("x1_dram", [TOKENS, DIM])
    persist.h2_dram = kept("h2_dram", [TOKENS, DIM])
    persist.slot_token = kept("slot_token", [SLOT_TILES * SLOTS, 1], I32)
    persist.y_dram = kept("y_dram", [SLOT_TILES * SLOTS, DIM])
    with ExitStack() as whole:
        persist.settled = whole.enter_context(nc.semaphore("settled"))

        def sb(stack, name, shape, dt=F32):
            return stack.enter_context(nc.sbuf_tensor(name, shape, dt))

        persist.wide_hi = sb(whole, "wide_hi", [P, KC, TOKENS], F32R)
        persist.wide_lo = sb(whole, "wide_lo", [P, KC, TOKENS], F32R)
        persist.ident = sb(whole, "ident", [P, P])
        persist.top_weight = sb(whole, "top_weight", [P, TT, 8])
        persist.slots = sb(whole, "slots", [P, TT, TOP], I32)
        persist.shared_gate = sb(whole, "shared_gate", [P, TT])
        persist.tile_expert = sb(whole, "tile_expert", [P, SLOT_TILES], I32)
        with ExitStack() as attending:
            persist.R = sb(attending, "R", [P, TT, 2 * DIM])
            with ExitStack() as values:
                persist.V = sb(values, "V", [P, TT, HEADS, HEAD + 1])
                norm_and_project(nc, persist, x, w_qkv_t, b_qkv, rope, c, w_mod_t)
                attention(nc, persist)
            norm_and_route(nc, persist, x, gates_t)
        persist.shared_sum = sb(whole, "shared_sum", [P, TT, DIM])
        shared_expert(nc, persist, w_shared_t)
        routed_experts(nc, persist, w_experts, w_tails)
        combine(nc, persist, out)


def rope_table():
    inv = (1.0 / np.float32(10000.0) ** (np.arange(0, HEAD, 2, dtype=np.float32) / np.float32(HEAD))).astype(np.float32)
    angle = np.arange(TOKENS, dtype=np.float32)[:, None] * inv[None, :]
    cos, sin = np.cos(angle), np.sin(angle)
    table = np.stack([np.concatenate([cos, cos], 1), np.concatenate([-sin, sin], 1)], 1)
    return np.ascontiguousarray(table.reshape(TT, P, 2, HEAD).transpose(1, 0, 2, 3).astype(np.float32))


def chunked(w):
    return np.ascontiguousarray(w.T.reshape(-1, P, w.shape[0]).transpose(1, 0, 2))


def layout(i):
    a = {}
    a['x'] = i['L0_attn_hidden_states'].reshape(TOKENS, DIM)
    w = i['L0_attn_w_qkv'].reshape(HEADS, 3, HEAD, DIM).transpose(1, 0, 2, 3).reshape(3 * DIM, DIM)
    a['w_qkv_t'] = chunked(w)
    a['b_qkv'] = i['L0_attn_b_qkv'].reshape(HEADS, 3, HEAD).transpose(1, 0, 2).reshape(3 * DIM)
    a['rope'] = rope_table()
    a['c'] = i['L0_c'].reshape(KC, P).T
    a['w_mod_t'] = i['L0_wmod'].reshape(KC, P, 6, DIM).transpose(1, 2, 0, 3)
    a['gates_t'] = chunked(np.concatenate([i['L0_ffn_gate_w'], i['L0_ffn_sgate_w']]))
    gu = i['L0_ffn_shared_gate_up_w'].reshape(2, SHARED // P, P, KC, P)
    gu = gu.transpose(1, 4, 3, 0, 2).reshape(SHARED // P, P, KC * 2 * P)
    down = i['L0_ffn_shared_down_w'].T.reshape(SHARED // P, P, DIM)
    a['w_shared_t'] = np.concatenate([gu, down], 2)
    w13 = i['L0_ffn_w13'].reshape(EXPERTS, 2, INNER, KC, P).transpose(0, 4, 3, 1, 2).reshape(EXPERTS, P, W13)
    w2 = i['L0_ffn_w2'].transpose(0, 2, 1)
    w2_wide = w2[:, :2 * P].reshape(EXPERTS, 2, P, DIM).transpose(0, 2, 1, 3).reshape(EXPERTS, P, 2 * DIM)
    a['w_experts'] = np.concatenate([w13, w2_wide], 2)
    a['w_tails'] = w2[:, 2 * P:]
    return a


_INS = ['x', 'w_qkv_t', 'b_qkv', 'rope', 'c', 'w_mod_t', 'gates_t', 'w_shared_t', 'w_experts', 'w_tails']


def kernel(**inputs):
    import concourse.bacc as _bacc
    from concourse.bass_utils import run_bass_kernel_spmd as _run

    nc = _bacc.Bacc("TRN2", target_bir_lowering=False, num_devices=1)
    laid = layout({name: np.asarray(a) for name, a in inputs.items()})
    arrays, args = {}, []
    for name in _INS:
        a = np.ascontiguousarray(laid[name])
        arrays[f"in_{name}"] = a
        args.append(nc.dram_tensor(f"in_{name}", a.shape, mybir.dt.from_np(a.dtype), kind="ExternalInput").ap())
    out = nc.dram_tensor("out", [TOKENS, DIM], F32, kind="ExternalOutput").ap()
    adaln_block(nc, *args, out)
    r = _run(nc, [arrays], core_ids=[0])
    return r.results[0]["out"].reshape(1, TOKENS, DIM)
```

```python
import numpy as np
import concourse.bass as bass
from concourse import mybir
from concourse.alu_op_type import AluOpType as ALU
from contextlib import ExitStack

F32 = mybir.dt.float32
F32R = mybir.dt.float32r
BF16 = mybir.dt.bfloat16
I32 = mybir.dt.int32
U32 = mybir.dt.uint32
ACT = mybir.ActivationFunctionType
X = mybir.AxisListType.X

P = 128
TOKENS = 2048
DIM = 512
HEADS = 16
HEAD = DIM // HEADS
KC = DIM // P
TT = TOKENS // P
EXPERTS = 16
TOP = 4
INNER = 352
SHARED = 1408
EPS = 1e-5
MASKED = -1e30


def staged(eng, n, stages, period=2, peeled=0):
    leads = [lead for _, lead in stages]
    start, end = peeled - min(leads), n - max(leads)
    end -= (end - start) % period

    def step(s):
        for stage, lead in stages:
            if 0 <= s + lead < n:
                stage(s + lead, (s + lead) % period)

    for s in range(-max(leads), start):
        step(s)
    with eng.Fori(0, (end - start) // period) as i:
        for u in range(period):
            for stage, lead in stages:
                stage(period * i + (start + u + lead), (start + u + lead) % period)
    for s in range(end, n - min(leads)):
        step(s)


def settle(eng, settled):
    eng.sem_inc(settled, 1)


def tile_of(ap, t):
    if isinstance(t, int):
        return ap[:, t]
    return ap[:, bass.ds(t, 1)].squeeze(1)


def rows_of(dram, t, rows=P):
    return dram[bass.ds(t * rows, rows), :]


def norm_and_project(nc, persist, x, w_qkv_t, b_qkv, rope, c, w_mod_t):
    ctx = ExitStack()
    with ctx:
        def sb(name, shape, dt=F32):
            return ctx.enter_context(nc.sbuf_tensor(name, shape, dt))

        def sem(name):
            return ctx.enter_context(nc.semaphore(name))

        E3 = 3 * DIM
        w_hi = persist.wide_hi[:, :, 0:E3]
        w_lo = persist.wide_lo[:, :, 0:E3]
        bias = sb("bias", [P, E3])
        rope_sb = sb("rope_sb", [P, TT, 2, HEAD])
        cvec = sb("cvec", [P, 4, KC])
        c_rows = sb("c_rows", [P, KC, P])
        x_sb = sb("x_sb", [P, 2, DIM])
        stats = sb("stats", [P, 6])
        mv = sb("mv", [P, 2])
        small = sb("small", [P, 4])
        h = sb("h", [P, 2, DIM])
        hT_hi = persist.wide_hi[:, 0:2, E3:E3 + DIM]
        hT_lo = persist.wide_lo[:, 0:2, E3:E3 + DIM]
        qk = sb("qk", [P, 2, 2 * DIM])
        qk_cos = sb("qk_cos", [P, 2, 2 * DIM])
        qk_sin = sb("qk_sin", [P, 2 * DIM])
        ps_t = [ctx.enter_context(nc.psum_tensor(f"ps_t{i}", [P, DIM], F32)) for i in range(2)]
        ps_qkv = [ctx.enter_context(nc.psum_tensor(f"ps_qkv{i}", [P, E3], F32)) for i in range(2)]
        first_mod = sb("first_mod", [P, 2, DIM])
        ps_mod = [ps_qkv[j // 3][:, (j % 3) * DIM:(j % 3 + 1) * DIM] for j in range(6)]
        later = qk[:].rearrange("p u (j n) -> p (u j) n", n=DIM)
        mod = [first_mod[:, 0], first_mod[:, 1], later[:, 0], later[:, 1], later[:, 2], later[:, 3]]
        ident = persist.ident
        R, V = persist.R, persist.V
        sgn, mag = qk_sin[:, 0:DIM], qk_sin[:, DIM:2 * DIM]
        flat_R = R[:].rearrange("p t n -> p (t n)")
        flat_V = V[:].rearrange("p t g f -> p (t g f)")
        w_raw = [flat_R[:, 8 * 2 * DIM + k * E3:8 * 2 * DIM + (k + 1) * E3] for k in range(KC)]
        w_mod = [flat_R[:, j * KC * DIM:(j + 1) * KC * DIM] for j in range(4)]
        w_mod += [flat_V[:, j * KC * DIM:(j + 1) * KC * DIM] for j in range(2)]

        c_loaded = sem("c_loaded")
        tables_loaded = sem("tables_loaded")
        wmod_loaded = [sem(f"wmod_loaded{i}") for i in range(6)]
        w_loaded = [sem(f"w_loaded{i}") for i in range(KC)]
        x_loaded = [sem(f"x_loaded{i}") for i in range(2)]
        c_exp = sem("c_exp")
        c_ready = sem("c_ready")
        mod_summed = sem("mod_summed")
        mod_ready = sem("mod_ready")
        w_hi_ready = sem("w_hi_ready")
        w_lo_ready = sem("w_lo_ready")
        var_ready = sem("var_ready")
        std_ready = sem("std_ready")
        xn_ready = sem("xn_ready")
        h_ready = sem("h_ready")
        hT_summed = sem("hT_summed")
        hT_hi_ready = sem("hT_hi_ready")
        hT_lo_ready = sem("hT_lo_ready")
        qkv_summed = sem("qkv_summed")
        qk_ready = sem("qk_ready")
        qkv_read = sem("qkv_read")
        cos_ready = sem("cos_ready")
        rotated = sem("rotated")
        vec_step = sem("vec_step")
        h_scaled = sem("h_scaled")
        ident_step = sem("ident_step")
        const_step = sem("const_step")
        gate_step = sem("gate_step")
        gates_ready = sem("gates_ready")
        mod_kept = sem("mod_kept")
        ident_ready = sem("ident_ready")

        block = ctx.enter_context(nc.Block())

        @block.sync
        def _(sync):
            sync.dma_start(cvec[:, 0, :], c).then_inc(c_loaded, 16)
            def load_mod(j):
                sync.dma_start(w_mod[j], w_mod_t[:, j].rearrange("p k n -> p (k n)")).then_inc(wmod_loaded[j], 16)

            for u in range(2):
                sync.dma_start(x_sb[:, u], rows_of(x, u)).then_inc(x_loaded[u], 16)
            for j in range(4):
                load_mod(j)
            for k in range(KC):
                sync.dma_start(w_raw[k], w_qkv_t[:, k]).then_inc(w_loaded[k], 16)
            load_mod(4)
            load_mod(5)
            sync.dma_start(bias[:], b_qkv.partition_broadcast(P)).then_inc(tables_loaded, 16)
            sync.dma_start(rope_sb[:], rope).then_inc(tables_loaded, 16)

            def load_x(t, u):
                sync.wait_ge(xn_ready, t - 1)
                sync.dma_start(x_sb[:, u], rows_of(x, t)).then_inc(x_loaded[u], 16)

            load_x(2, 0)
            load_x(3, 1)
            sync.wait_ge(gates_ready, 2)
            sync.wait_ge(mod_ready, 6)
            sync.dma_start(persist.mod_dram, later).then_inc(mod_kept, 16)
            with sync.Fori(1, TT // 2 - 1) as i:
                for u in (0, 1):
                    load_x(2 * i + u + 2, u)

        @block.gpsimd
        def _(pool):
            nc.gpsimd.memset(ident[:], 0.0).then_inc(ident_step, 1)
            pool.wait_ge(ident_step, 1)
            nc.gpsimd.affine_select(out=ident[:], in_=ident[:], compare_op=ALU.not_equal, fill=1.0, base=0,
                                    pattern=[[-1, P]], channel_multiplier=1).then_inc(ident_ready, 1)
            ident_bf, mask, own_tile = persist.ident_bf, persist.mask, persist.own_tile
            nc.gpsimd.memset(ident_bf[:], 0.0).then_inc(const_step, 1)
            nc.gpsimd.memset(mask[:], 0.0).then_inc(const_step, 1)
            nc.gpsimd.memset(own_tile[:], 0.0).then_inc(const_step, 1)
            pool.wait_ge(const_step, 3)
            nc.gpsimd.affine_select(out=ident_bf[:], in_=ident_bf[:], compare_op=ALU.not_equal, fill=1.0, base=0,
                                    pattern=[[-1, P]], channel_multiplier=1)
            nc.gpsimd.affine_select(out=mask[:], in_=mask[:], compare_op=ALU.is_ge, fill=MASKED, base=0,
                                    pattern=[[-1, P]], channel_multiplier=1)
            for part in range(2):
                nc.gpsimd.affine_select(out=own_tile[:], in_=own_tile[:], compare_op=ALU.not_equal, fill=1.0,
                                        base=-TT * part, pattern=[[-1, TT]],
                                        channel_multiplier=1).then_inc(const_step, 1)
                pool.wait_ge(const_step, 4 + part)
            pool.wait_ge(mod_ready, 2)

            def modulate(t, u):
                pool.wait_ge(xn_ready, t + 1)
                nc.gpsimd.tensor_tensor(h[:, u], h[:, u], mod[1], ALU.mult).then_inc(h_scaled, 1)
                pool.wait_ge(h_scaled, t + 1)
                nc.gpsimd.tensor_tensor(h[:, u], h[:, u], mod[0], ALU.add).then_inc(h_ready, 1)

            def times_cos(t, u):
                if isinstance(t, int) and t == 0:
                    pool.wait_ge(tables_loaded, 32)
                pool.wait_ge(qk_ready, t + 1)
                settle(pool, persist.settled)
                cos = tile_of(rope_sb[:, :, 0], t).unsqueeze(1).to_broadcast([P, 2 * HEADS, HEAD])
                nc.gpsimd.tensor_tensor(qk_cos[:, u].rearrange("p (g f) -> p g f", f=HEAD),
                                        qk[:, u].rearrange("p (g f) -> p g f", f=HEAD), cos,
                                        ALU.mult).then_inc(cos_ready, 1)

            staged(pool, TT, [(modulate, 2), (times_cos, -1)], peeled=1)

        @block.scalar
        def _(act):
            act.wait_ge(c_loaded, 16)
            nc.scalar.activation(cvec[:, 1], cvec[:, 0], ACT.Exp, scale=-1.0).then_inc(c_exp, 1)

            def evacuate_mod(j):
                act.wait_ge(mod_summed, j + 1)
                nc.scalar.activation(mod[j], ps_mod[j], ACT.Copy,
                                     bias=1.0 if j in (1, 4) else 0.0).then_inc(mod_ready, 1)

            evacuate_mod(0)
            evacuate_mod(1)
            def std(t, u):
                act.wait_ge(var_ready, t + 1)
                nc.scalar.activation(small[:, 1:2], small[:, 0:1], ACT.Sqrt).then_inc(std_ready, 1)
                if isinstance(t, int) and t == 1:
                    for k in range(KC):
                        act.wait_ge(w_loaded[k], 16)
                        nc.scalar.activation(w_hi[:, k], w_raw[k], ACT.Copy).then_inc(w_hi_ready, 1)

            def split_hi(t, u):
                act.wait_ge(hT_summed, t + 1)
                nc.scalar.activation(hT_hi[:, u], ps_t[u][:], ACT.Copy).then_inc(hT_hi_ready, 1)
                if isinstance(t, int) and t == 0:
                    for j in range(2, 6):
                        evacuate_mod(j)

            staged(act, TT, [(std, 2), (split_hi, 1)], peeled=1)

        @block.vector
        def _(vec):
            vec.wait_ge(c_exp, 1)
            nc.vector.tensor_scalar(cvec[:, 2], cvec[:, 1], 1.0, None, ALU.add).then_inc(vec_step, 1)
            vec.wait_ge(vec_step, 1)
            nc.vector.reciprocal(cvec[:, 2], cvec[:, 2]).then_inc(vec_step, 1)
            vec.wait_ge(vec_step, 2)
            nc.vector.tensor_tensor(cvec[:, 3], cvec[:, 2], cvec[:, 0], ALU.mult).then_inc(vec_step, 1)
            vec.wait_ge(vec_step, 3)
            nc.vector.tensor_copy(c_rows[:], cvec[:, 3].unsqueeze(2).to_broadcast([P, KC, P])).then_inc(c_ready, 1)
            base = 3
            NORM_STEPS = 3

            def normalise(t, u):
                s = base + t * NORM_STEPS
                vec.wait_ge(x_loaded[u], 16 * ((t - u) // 2 + 1) if isinstance(t, int) else (t - u) * 8 + 16)
                nc.vector.bn_stats(stats[:], x_sb[:, u]).then_inc(vec_step, 1)
                vec.wait_ge(vec_step, s + 1)
                settle(vec, persist.settled)
                nc.vector.bn_aggr(mv[:], stats[:]).then_inc(vec_step, 1)
                vec.wait_ge(vec_step, s + 2)
                nc.vector.tensor_scalar(small[:, 0:1], mv[:, 1:2], EPS, None, ALU.add).then_inc(var_ready, 1)
                vec.wait_ge(std_ready, t + 1)
                nc.vector.reciprocal(small[:, 2:3], small[:, 1:2]).then_inc(vec_step, 1)
                vec.wait_ge(vec_step, s + 3)
                nc.vector.tensor_scalar(h[:, u], x_sb[:, u], mv[:, 0:1], small[:, 2:3],
                                        ALU.subtract, ALU.mult).then_inc(xn_ready, 1)
                if isinstance(t, int) and t == 1:
                    for k in range(KC):
                        vec.wait_ge(w_hi_ready, k + 1)
                        nc.vector.tensor_tensor(w_lo[:, k], w_raw[k], w_hi[:, k].bitcast(F32),
                                                ALU.subtract).then_inc(w_lo_ready, 1)

            def split_lo(t, u):
                vec.wait_ge(hT_hi_ready, t + 1)
                nc.vector.tensor_tensor(hT_lo[:, u], ps_t[u][:], hT_hi[:, u].bitcast(F32),
                                        ALU.subtract).then_inc(hT_lo_ready, 1)
                if isinstance(t, int) and t == 1:
                    gates()

            def gates():
                for n, j in enumerate((2, 5)):
                    vec.wait_ge(mod_ready, j + 1)
                    nc.vector.tensor_scalar(sgn, mod[j], 0.0, 2.0, ALU.is_ge, ALU.mult).then_inc(gate_step, 1)
                    nc.vector.scalar_tensor_tensor(mag, mod[j], -1.0, mod[j], ALU.mult, ALU.max).then_inc(gate_step, 1)
                    vec.wait_ge(gate_step, 3 * n + 2)
                    nc.vector.tensor_scalar(mag, mag, 0.25, None, ALU.max).then_inc(gate_step, 1)
                    vec.wait_ge(gate_step, 3 * n + 3)
                    nc.vector.scalar_tensor_tensor(mod[j], sgn, -1.0, mag, ALU.add, ALU.mult).then_inc(gates_ready, 1)
                    vec.wait_ge(gates_ready, n + 1)

            def add_bias(t, u):
                if isinstance(t, int) and t == 0:
                    vec.wait_ge(mod_kept, 16)
                    vec.wait_ge(tables_loaded, 32)
                vec.wait_ge(qkv_summed, t + 1)
                nc.vector.tensor_tensor(qk[:, u], ps_qkv[u][:, 0:2 * DIM], bias[:, 0:2 * DIM],
                                        ALU.add).then_inc(qk_ready, 1)
                nc.vector.tensor_tensor(tile_of(V, t)[:, :, 0:HEAD],
                                        ps_qkv[u][:, 2 * DIM:].rearrange("p (g f) -> p g f", f=HEAD),
                                        bias[:, 2 * DIM:].rearrange("p (g f) -> p g f", f=HEAD),
                                        ALU.add).then_inc(qkv_read, 1)

            def rotate(t, u):
                half = HEAD // 2
                vec.wait_ge(qk_ready, t + 1)
                src = qk[:, u].rearrange("p (g f) -> p g f", f=HEAD)
                dst = qk_sin[:].rearrange("p (g f) -> p g f", f=HEAD)
                sin = tile_of(rope_sb[:, :, 1], t)
                if not (isinstance(t, int) and t == 0):
                    vec.wait_ge(rotated, 2 * t)
                nc.vector.tensor_tensor(dst[:, :, 0:half], src[:, :, half:],
                                        sin[:, 0:half].unsqueeze(1).to_broadcast([P, 2 * HEADS, half]), ALU.mult)
                nc.vector.tensor_tensor(dst[:, :, half:], src[:, :, 0:half],
                                        sin[:, half:].unsqueeze(1).to_broadcast([P, 2 * HEADS, half]),
                                        ALU.mult).then_inc(rotated, 1)
                vec.wait_ge(rotated, 2 * t + 1)
                vec.wait_ge(cos_ready, t + 1)
                nc.vector.tensor_tensor(tile_of(R, t), qk_cos[:, u], qk_sin[:], ALU.add).then_inc(rotated, 1)

            staged(vec, TT, [(normalise, 2), (split_lo, 1), (add_bias, -1), (rotate, -2)], peeled=1)
            nc.vector.memset(V[:, :, :, HEAD:HEAD + 1], 1.0)

        @block.tensor
        def _(pe):
            pe.wait_ge(c_ready, 1)

            def modulation(j):
                pe.wait_ge(wmod_loaded[j], 16)
                for k in range(KC):
                    last = nc.tensor.matmul(ps_mod[j], c_rows[:, k], w_mod[j][:, k * DIM:(k + 1) * DIM],
                                            start=k == 0, stop=k == KC - 1)
                last.then_inc(mod_summed, 1)

            for j in range(4):
                modulation(j)
            pe.wait_ge(ident_ready, 1)

            def transpose_h(t, u):
                pe.wait_ge(h_ready, t + 1)
                for k in range(KC):
                    last = nc.tensor.transpose(ps_t[u][:, k * P:(k + 1) * P], h[:, u, k * P:(k + 1) * P], ident[:])
                last.then_inc(hT_summed, 1)
                if isinstance(t, int) and t == 0:
                    modulation(4)
                    modulation(5)

            def project(t, u):
                if isinstance(t, int) and t == 0:
                    pe.wait_ge(mod_ready, 6)
                    pe.wait_ge(w_lo_ready, KC)
                pe.wait_ge(hT_lo_ready, t + 1)
                pe.wait_ge(qkv_read, t + 1)
                for n in range(3):
                    for k in range(KC):
                        ks = slice(k * P, (k + 1) * P)
                        ns = slice(n * DIM, (n + 1) * DIM)
                        for m, (a, b) in enumerate(((hT_lo, w_hi), (hT_hi, w_lo), (hT_hi, w_hi))):
                            last = nc.tensor.matmul(ps_qkv[u][:, ns], a[:, u, ks], b[:, k, ns],
                                                    start=k == 0 and m == 0, stop=k == KC - 1 and m == 2)
                last.then_inc(qkv_summed, 1)

            pe.sem_inc(qkv_read, 2)
            staged(pe, TT, [(transpose_h, 1), (project, 0)], peeled=1)



PAIRS = HEADS // 2
AHEAD = 1.06
BEHIND_SLICE = 1.5
SLICE = 4
STACK = 3 * HEAD


def prepare_events():
    GROUPS = TT // SLICE
    groups = [(hh, g) for hh in range(2) for g in range(GROUPS)]
    turn = [[("T", dict(hh=hh, kind=kind, g=g)) for kind in range(2)] for hh, g in groups] + [[]]
    events, m = list(turn[0]), 0
    for (hh, g), coming in zip(groups, turn[1:]):
        scores = []
        for qt in range(SLICE * g, SLICE * g + SLICE):
            end = (qt + 1) * P
            for n, start in enumerate(range(0, end, DIM)):
                stop = min(start + DIM, end)
                wide = start if stop - start >= 2 * P or start == 0 else start - P
                scores.append(("M", dict(hh=hh, g=g, qt=qt, n=n, start=start, stop=stop, wide=wide, m=m)))
                m += 1
        if hh == 1 and g == 0:
            places = ((4, coming[1]), (2, ("N", dict(hh=0))), (1, coming[0]))
        else:
            places = tuple(zip((len(scores) // 2 + 1, 1), reversed(coming)))
        for place, event in places:
            scores.insert(place, event)
        events += scores
        if g == GROUPS - 1:
            events.append(("R", dict(hh=hh, seen=m)))
    return events + [("N", dict(hh=1))], m


def attend_events(first=False, last=False):
    events, b, blocks = [], 0, []
    for s in range(TT // SLICE):
        for kt in range(SLICE * (s + 1)):
            blocks.append(dict(b=b, s=s, kt=kt, skip=max(0, kt - SLICE * s) * P, last=kt == SLICE * (s + 1) - 1))
            b += 1
    late = {} if first else {2: dict(s=TT // SLICE - 1, carried=True)}
    for n in range(len(blocks) + 1):
        if n < len(blocks):
            events.append(("S", blocks[n]))
        if n in late:
            events.append(("O", late[n]))
        if n:
            events.append(("A", blocks[n - 1]))
            if blocks[n - 1]["last"]:
                events.append(("E", dict(s=blocks[n - 1]["s"], blocks=n)))
                late[n + 2] = dict(s=blocks[n - 1]["s"])
    if last:
        events += [("O", e) for n, e in late.items() if n > len(blocks)]
    return events, b


def merged(prepare, attend):
    def cost(kind, e):
        return max(e["stop"] - e["wide"], P) / DIM + 0.1 if kind == "M" else {"T": 0.4, "N": 0.4, "R": 0.8}[kind]

    def share(kind, e):
        return {"S": 0.35, "A": 0.65}.get(kind, 0.0) * (1 - e["skip"] / DIM / 2) if kind in "SA" else 0.0

    total, work = sum(cost(k, e) for k, e in prepare), sum(share(k, e) for k, e in attend)
    out, left, spent, done = [], list(prepare), 0.0, 0.0
    for kind, e in attend:
        out.append((kind, e))
        done += share(kind, e) / work
        more = BEHIND_SLICE if kind == "E" else 0.0
        while left and spent < total * min(1.0, done * AHEAD) + more:
            spent += cost(*left[0])
            out.append(left.pop(0))
    return out + left


def numbered(events):
    out, use, turned = [], 0, {}
    for kind, e in events:
        out.append((kind, dict(e, use=use, turned=turned.get((e["hh"], e["g"])) if kind == "M" else 0)))
        use += kind in "TNO"
        if kind == "T":
            turned[e["hh"], e["g"]] = use
    return out, use


def attention(nc, persist):
    prepare, M_UNITS = prepare_events()
    first, BLOCKS = attend_events(first=True)
    first, _ = numbered(merged(prepare, first))
    both, STEP_USES = numbered(merged(prepare, attend_events()[0]))
    last, _ = numbered(attend_events(last=True)[0])
    prepare, FIRST_USES = numbered(prepare)
    SLICES = TT // SLICE
    CREDITS = 2
    ctx = ExitStack()
    with ctx:
        def sb(name, shape, dt=F32):
            return ctx.enter_context(nc.sbuf_tensor(name, shape, dt))

        def psum(name, shape):
            return ctx.enter_context(nc.psum_tensor(name, shape, F32))

        def sem(name):
            return ctx.enter_context(nc.semaphore(name))

        R, V, ident = persist.R, persist.V, persist.ident
        ident_bf, mask, own_tile = persist.ident_bf, persist.mask, persist.own_tile
        qT = [[persist.wide_hi[:, 2 * i + j] for j in range(2)] for i in range(2)]
        kT = [[persist.wide_lo[:, 2 * i + j] for j in range(2)] for i in range(2)]
        stack = [[sb(f"{name}_stack{hh}", [P, TT, STACK], F32R) for name in "kq"] for hh in range(2)]
        v_pair = [sb(f"v_pair{i}", [P, TT, 2, HEAD + 1]) for i in range(2)]
        probs = [sb(f"probs{i}", [P, 2, DIM]) for i in range(2)]
        part_max = sb("part_max", [P, TT, SLICE])
        row_max = sb("row_max", [P, TT])
        neg_max = sb("neg_max", [P, 2, TT], F32R)
        o_sb = sb("o_sb", [HEAD + 1, 2, DIM])
        max_rows = persist.top_weight[0:32].rearrange("p t n -> p (t n)")
        o_inv = sb("o_inv", [P, SLICE, 2, 1])
        ps_s = [psum(f"ps_s{i}", [P, 2, DIM]) for i in range(2)]
        ps_m = [psum(f"ps_m{i}", [P, DIM]) for i in range(2)]
        ps_o = psum("ps_o", [P, DIM])
        ps_x = psum("ps_x", [P, DIM])

        rows_set = sem("rows_set")
        part_set = sem("part_set")
        stack_ready = sem("stack_ready")
        v_ready = sem("v_ready")
        x_ready = sem("x_ready")
        x_taken = sem("x_taken")
        m_ready = sem("m_ready")
        m_taken = sem("m_taken")
        max_step = sem("max_step")
        neg_ready = sem("neg_ready")
        spread_done = sem("spread_done")
        s_ready = sem("s_ready")
        p_ready = sem("p_ready")
        p_used = sem("p_used")
        o_taken = sem("o_taken")
        inv_ready = sem("inv_ready")
        block = ctx.enter_context(nc.Block())

        BUILD = 6

        def build(eng, q, hh):
            done = (q * 2 + hh) * BUILD
            for kind, (parts, low) in enumerate((((0, 1), 2), ((0, 2), 1))):
                col = (1 - kind) * DIM + q * (2 * HEAD) + hh * HEAD
                src = R[:, :, bass.ds(col, HEAD)]
                dst = [stack[hh][kind][:, :, n * HEAD:(n + 1) * HEAD] for n in range(3)]
                for n in parts:
                    eng.tensor_copy(dst[n], src).then_inc(stack_ready, 1)
                eng.wait_ge(stack_ready, done + 3 * kind + 2)
                settle(eng, persist.settled)
                eng.tensor_tensor(dst[low], src, dst[0].bitcast(F32), ALU.subtract).then_inc(stack_ready, 1)

        def spread(eng, u, hh, rows):
            return eng.tensor_tensor(qT[u][hh][STACK:P, :].rearrange("p (t n) -> p t n", n=P),
                                     rows.unsqueeze(1).to_broadcast([32, TT, P]),
                                     own_tile[:].unsqueeze(2).to_broadcast([32, TT, P]), ALU.mult)

        def walk(handle):
            def run(eng):
                def step(p, u, events):
                    for kind, e in events:
                        ahead = FIRST_USES + e["use"] if events is first else p * STEP_USES + (FIRST_USES - 1 + e["use"])
                        if kind in "TMRN":
                            handle(eng, kind, p + 1, 1 - u, e, ahead)
                        elif "carried" in e:
                            handle(eng, kind, p - 1, 1 - u, e, ahead)
                        else:
                            handle(eng, kind, p, u, e, ahead)

                for kind, e in prepare:
                    handle(eng, kind, 0, 0, e, e["use"])
                step(0, 0, first)
                with eng.Fori(0, PAIRS // 2 - 2) as i:
                    for u in (1, 0):
                        step(2 * i + (2 - u), u, both)
                step(PAIRS - 3, 1, both)
                step(PAIRS - 2, 0, both)
                step(PAIRS - 1, 1, last)
            return run

        @block.gpsimd
        def _(pool):
            def handle(eng, kind, q, u, e, ahead):
                if kind == "T" and e["g"] == TT // SLICE - 1 and e["kind"] == 1:
                    eng.wait_ge(x_ready, ahead + 1)
                    if e["hh"] == 0:
                        nc.gpsimd.tensor_copy(v_pair[u][:], V[:, :, bass.ds(q * 2, 2), :]).then_inc(v_ready, 1)
                    if e["hh"] == 1:
                        eng.wait_ge(spread_done, q + 1)
                    if not isinstance(q, int) or q < PAIRS - 1:
                        build(nc.gpsimd, q + 1, e["hh"])
                elif kind == "N" and e["hh"] == 0:
                    last_pair = isinstance(q, int) and q == PAIRS - 1
                    eng.wait_ge(stack_ready, 2 * PAIRS * BUILD if last_pair else q * (2 * BUILD) + 3 * BUILD)
                    eng.wait_ge(v_ready, q + 1)
                    eng.wait_ge(x_taken, ahead + 1)
                    spread(nc.gpsimd, u, 0, max_rows).then_inc(spread_done, 1)

            for i in range(2):
                for j in range(2):
                    nc.gpsimd.memset(kT[i][j][STACK:P, :].bitcast(F32), 1.0).then_inc(rows_set, 1)
            pool.wait_ge(rows_set, 4)
            pool.wait_ge(stack_ready, BUILD)
            build(nc.gpsimd, 0, 1)
            walk(handle)(pool)

        @block.scalar
        def _(act):
            def handle(eng, kind, q, u, e, ahead):
                if kind == "T":
                    g = e["g"]
                    dst = (kT, qT)[e["kind"]][u][e["hh"]][0:STACK, g * DIM:(g + 1) * DIM]
                    eng.wait_ge(x_ready, ahead + 1)
                    nc.scalar.activation(dst, ps_x[0:STACK, :], ACT.Copy).then_inc(x_taken, 1)
                elif kind == "S":
                    b, n = e["b"] % 2, q * BLOCKS + e["b"]
                    eng.wait_ge(s_ready, n + 1)
                    eng.wait_ge(p_used, n + 1)
                    nc.scalar.activation(probs[b][:, :, e["skip"]:], ps_s[b][:, :, e["skip"]:], ACT.Exp,
                                         scale=HEAD ** -0.5).then_inc(p_ready, 1)
                elif kind == "E":
                    eng.wait_ge(p_used, q * BLOCKS + (e["blocks"] + CREDITS))
                    eng.wait_ge(x_ready, ahead)
                    nc.scalar.activation(o_sb[:, 0], ps_o[0:HEAD + 1, :], ACT.Copy).then_inc(o_taken, 1)

            walk(handle)(act)

        @block.vector
        def _(vec):
            build(nc.vector, 0, 0)
            nc.vector.memset(part_max[:], -3e38).then_inc(part_set, 1)
            vec.wait_ge(part_set, 1)

            def handle(eng, kind, q, u, e, ahead):
                if kind == "M":
                    m = q * M_UNITS + e["m"]
                    eng.wait_ge(m_ready, m + 1)
                    nc.vector.reduce_max(part_max[:, e["qt"], e["n"]:e["n"] + 1],
                                         ps_m[e["m"] % 2][:, e["start"] - e["wide"]:e["stop"] - e["wide"]],
                                         X).then_inc(m_taken, 1)
                elif kind == "R":
                    head = q * 2 + e["hh"]
                    eng.wait_ge(m_taken, q * M_UNITS + (e["seen"] + CREDITS))
                    nc.vector.reduce_max(row_max[:], part_max[:], X).then_inc(max_step, 1)
                    eng.wait_ge(max_step, head * 2 + 1)
                    nc.vector.tensor_scalar(neg_max[:, 0], row_max[:], -1.0, None, ALU.mult).then_inc(max_step, 1)
                    eng.wait_ge(max_step, head * 2 + 2)
                    nc.vector.scalar_tensor_tensor(neg_max[:, 1], row_max[:], -1.0, neg_max[:, 0].bitcast(F32),
                                                   ALU.mult, ALU.subtract).then_inc(neg_ready, 1)
                elif kind == "N":
                    eng.wait_ge(x_ready, ahead + 1)
                    if e["hh"] == 0:
                        if not (isinstance(q, int) and q == 0):
                            eng.wait_ge(spread_done, q)
                        nc.vector.tensor_copy(max_rows, ps_x[0:32, 0:P]).then_inc(x_taken, 1)
                    else:
                        spread(nc.vector, u, 1, ps_x[0:32, 0:P]).then_inc(x_taken, 1)
                elif kind == "E":
                    eng.wait_ge(p_used, q * BLOCKS + (e["blocks"] + CREDITS))
                    eng.wait_ge(x_ready, ahead)
                    nc.vector.tensor_copy(o_sb[:, 1], ps_o[64:64 + HEAD + 1, :]).then_inc(o_taken, 1)
                elif kind == "O":
                    s = e["s"]
                    eng.wait_ge(x_ready, ahead + 1)
                    o = ps_x[:, 0:SLICE * 2 * (HEAD + 1)].rearrange("p (j h f) -> p j h f", h=2, f=HEAD + 1)
                    nc.vector.reciprocal(o_inv[:], o[:, :, :, HEAD:]).then_inc(inv_ready, 1)
                    eng.wait_ge(inv_ready, q * SLICES + (s + 1))
                    dst = R[:, SLICE * s:SLICE * (s + 1), bass.ds(q * (2 * HEAD), 2 * HEAD)]
                    nc.vector.tensor_tensor(dst.rearrange("p j (h f) -> p j h f", h=2), o[:, :, :, 0:HEAD],
                                            o_inv[:].to_broadcast([P, SLICE, 2, HEAD]), ALU.mult).then_inc(x_taken, 1)

            walk(handle)(vec)

        @block.tensor
        def _(pe):
            pe.sem_inc(m_taken, CREDITS)
            pe.sem_inc(p_ready, CREDITS)
            pe.sem_inc(p_used, CREDITS)
            def handle(eng, kind, q, u, e, ahead):
                if kind in "TNO":
                    eng.wait_ge(x_taken, ahead)
                if kind == "T":
                    if e["g"] == 0 and e["kind"] == 0:
                        eng.wait_ge(stack_ready, (q * 2 + (e["hh"] + 1)) * 6)
                    for j in range(SLICE):
                        last = nc.tensor.transpose(ps_x[0:STACK, j * P:(j + 1) * P],
                                                   stack[e["hh"]][e["kind"]][:, SLICE * e["g"] + j, :].bitcast(F32), ident[:])
                    last.then_inc(x_ready, 1)
                elif kind == "M":
                    m, start, stop = q * M_UNITS + e["m"], e["wide"], e["stop"]
                    qs = slice(e["qt"] * P, (e["qt"] + 1) * P)
                    bank = ps_m[e["m"] % 2]
                    diagonal = stop == (e["qt"] + 1) * P
                    eng.wait_ge(x_taken, ahead - e["use"] + e["turned"])
                    eng.wait_ge(m_taken, m + 1)
                    last = nc.tensor.matmul(bank[:, 0:stop - start], qT[u][e["hh"]][0:STACK, qs],
                                            kT[u][e["hh"]][0:STACK, start:stop], start=True, stop=not diagonal)
                    if diagonal:
                        last = nc.tensor.matmul(bank[:, stop - start - P:stop - start], ident_bf[:], mask[:],
                                                start=False, stop=True)
                    last.then_inc(m_ready, 1)
                elif kind == "N":
                    eng.wait_ge(neg_ready, q * 2 + (e["hh"] + 1))
                    nc.tensor.transpose(ps_x[0:32, 0:P], neg_max[:].rearrange("p a t -> p (a t)").bitcast(F32),
                                        ident[:]).then_inc(x_ready, 1)
                elif kind == "S":
                    b, n, skip = e["b"] % 2, q * BLOCKS + e["b"], e["skip"]
                    if e["b"] == 0:
                        eng.wait_ge(rows_set, 4)
                        eng.wait_ge(spread_done, q + 1)
                        eng.wait_ge(x_taken, ahead)
                        eng.wait_ge(v_ready, q + 1)
                    eng.wait_ge(p_ready, n + 1)
                    qs = slice(e["s"] * DIM + skip, (e["s"] + 1) * DIM)
                    diagonal = e["kt"] >= SLICE * e["s"]
                    for hh in range(2):
                        last = nc.tensor.matmul(ps_s[b][:, hh, skip:], kT[u][hh][:, e["kt"] * P:(e["kt"] + 1) * P],
                                                qT[u][hh][:, qs], start=True, stop=not diagonal)
                        if diagonal:
                            last = nc.tensor.matmul(ps_s[b][:, hh, skip:skip + P], mask[:], ident_bf[:],
                                                    start=False, stop=True)
                    last.then_inc(s_ready, 1)
                elif kind == "A":
                    b, n, skip = e["b"] % 2, q * BLOCKS + e["b"], e["skip"]
                    eng.wait_ge(p_ready, n + (1 + CREDITS))
                    if e["kt"] == 0:
                        eng.wait_ge(o_taken, (q * SLICES + e["s"]) * 2)
                    for hh in range(2):
                        last = nc.tensor.matmul(ps_o[64 * hh:64 * hh + HEAD + 1, skip:], v_pair[u][:, e["kt"], hh, :],
                                                probs[b][:, hh, skip:], start=e["kt"] == 0, stop=e["last"])
                    last.then_inc(p_used, 1)
                elif kind == "O":
                    eng.wait_ge(o_taken, (q * SLICES + (e["s"] + 1)) * 2)
                    settle(eng, persist.settled)
                    for j in range(SLICE):
                        for hh in range(2):
                            at = (j * 2 + hh) * (HEAD + 1)
                            last = nc.tensor.transpose(ps_x[:, at:at + HEAD + 1], o_sb[:, hh, j * P:(j + 1) * P],
                                                       ident[0:HEAD + 1, 0:HEAD + 1])
                    last.then_inc(x_ready, 1)

            walk(handle)(pe)



SLOTS = 2 * P
SLOT_TILES = (TOKENS * TOP - EXPERTS) // SLOTS + EXPERTS
MOST = TOKENS // SLOTS
LOGITS = EXPERTS + 1


def norm_and_route(nc, persist, x, gates_t):
    ctx = ExitStack()
    with ctx:
        def sb(name, shape, dt=F32):
            return ctx.enter_context(nc.sbuf_tensor(name, shape, dt))

        def sem(name):
            return ctx.enter_context(nc.semaphore(name))

        R, ident = persist.R, persist.ident
        h2T_hi, h2T_lo = persist.wide_hi, persist.wide_lo
        mod = sb("mod2", [P, 3, DIM])
        gate_raw = sb("gate_raw", [P, KC, LOGITS])
        gate_hi = sb("gate_hi", [P, KC, LOGITS], F32R)
        gate_lo = sb("gate_lo", [P, KC, LOGITS], F32R)
        x_in = sb("x_in", [P, 2, DIM])
        x1 = sb("x1", [P, 2, DIM])
        h2 = sb("h2", [P, 2, DIM])
        stats = sb("stats2", [P, 6])
        mv = sb("mv2", [P, 2])
        small = sb("small2", [P, 4])
        logitsT = sb("logitsT", [LOGITS, TOKENS])
        logits = sb("logits", [P, TT, LOGITS])
        top_logit = sb("top_logit", [P, TT, 1])
        shifted = sb("shifted", [P, TT, EXPERTS])
        exps = sb("exps", [P, TT, EXPERTS])
        exp_sum = sb("exp_sum", [P, TT, 1])
        exp_inv = sb("exp_inv", [P, TT, 1])
        routing = sb("routing", [P, TT, EXPERTS])
        gate_exp = sb("gate_exp", [P, TT])
        top_index = sb("top_index", [P, TT, 8], U32)
        top_number = sb("top_number", [P, TT, TOP])
        chosen = sb("chosen", [P, TT, TOP, EXPERTS])
        picked = sb("picked", [P, TT, TOP, EXPERTS])
        member = sb("member", [P, TT, EXPERTS], BF16)
        counts = sb("counts", [P, EXPERTS, 1])
        above = sb("above", [P, EXPERTS, MOST])
        n_tiles = sb("n_tiles", [P, 1, EXPERTS])
        earlier = sb("earlier", [P, EXPERTS, EXPERTS])
        first_tile = sb("first_tile", [P, EXPERTS])
        end_tile = sb("end_tile", [P, 1, EXPERTS])
        first_slot = sb("first_slot", [P, 1, EXPERTS])
        slot_of = sb("slot_of", [P, TT, EXPERTS])
        slot_number = sb("slot_number", [P, TT, TOP])
        passed = sb("passed", [P, SLOT_TILES, EXPERTS])
        tile_number = sb("tile_number", [P, SLOT_TILES])
        expert_iota = sb("expert_iota", [P, EXPERTS])
        full_iota = sb("full_iota", [P, 1, MOST])
        tile_iota = sb("tile_iota", [P, SLOT_TILES, 1])
        before = sb("before", [P, EXPERTS, EXPERTS])
        earlier_tok = sb("earlier_tok", [P, P], BF16)
        ones_bf = sb("ones_bf", [P, P], BF16)
        empty_slot = sb("empty_slot", [SLOT_TILES, SLOTS, 2], I32)
        zeros = sb("zeros", [P, DIM])
        ps_t = [ctx.enter_context(nc.psum_tensor(f"ps_h{i}", [P, DIM], F32)) for i in range(2)]
        ps_l = [ctx.enter_context(nc.psum_tensor(f"ps_l{i}", [P, DIM], F32)) for i in range(2)]
        ps_g = ctx.enter_context(nc.psum_tensor("ps_g", [P, TT, LOGITS], F32))
        ps_pos = ctx.enter_context(nc.psum_tensor("ps_pos", [P, TT, EXPERTS], F32))
        ps_count = ctx.enter_context(nc.psum_tensor("ps_count", [P, EXPERTS, 1], F32))

        consts_loaded = sem("consts_loaded")
        x_loaded = [sem(f"x_in_loaded{i}") for i in range(2)]
        gate_hi_ready = sem("gate_hi_ready")
        gate_lo_ready = sem("gate_lo_ready")
        scaled = sem("scaled")
        x1_ready = sem("x1_ready")
        x1_stored = [sem(f"x1_stored{i}") for i in range(2)]
        h2_stored = [sem(f"h2_stored{i}") for i in range(2)]
        norm_step = sem("norm_step")
        var_ready = sem("var2_ready")
        std_ready = sem("std2_ready")
        xn_ready = sem("xn2_ready")
        h2_scaled = sem("h2_scaled")
        h2_ready = sem("h2_ready")
        h2T_summed = sem("h2T_summed")
        hi_ready = sem("h2T_hi_ready")
        lo_ready = sem("h2T_lo_ready")
        logitsT_summed = sem("logitsT_summed")
        logitsT_ready = sem("logitsT_ready")
        logits_turned = sem("logits_turned")
        shifted_ready = sem("shifted_ready")
        exps_ready = sem("exps_ready")
        route_step = sem("route_step")
        member_ready = sem("member_ready")
        counted = sem("counted")
        const_step = sem("const2_step")
        const_ready = sem("const2_ready")
        zeros_ready = sem("zeros_ready")
        rows_cleared = sem("rows_cleared")
        cleared = sem("cleared")
        block = ctx.enter_context(nc.Block())

        @block.sync
        def _(sync):
            sync.dma_start(mod[:], persist.mod_dram[:, 0:3]).then_inc(consts_loaded, 16)
            sync.dma_start(gate_raw[:], gates_t).then_inc(consts_loaded, 16)
            for u in range(2):
                sync.dma_start(x_in[:, u], rows_of(x, u)).then_inc(x_loaded[u], 16)
            with sync.Fori(0, TT // 2 - 1) as i:
                for u in (0, 1):
                    sync.wait_ge(x1_ready, 2 * i + u + 1)
                    sync.dma_start(rows_of(persist.out, 2 * i + u), x1[:, u]).then_inc(x1_stored[u], 16)
                    sync.dma_start(x_in[:, u], rows_of(x, 2 * i + u + 2)).then_inc(x_loaded[u], 16)
            for u in range(2):
                sync.wait_ge(x1_ready, TT - 2 + u + 1)
                sync.dma_start(rows_of(persist.out, TT - 2 + u), x1[:, u]).then_inc(x1_stored[u], 16)
            sync.wait_ge(zeros_ready, 1)
            for rows in (persist.out, persist.h2_dram):
                for c in range(SLOTS // P):
                    sync.dma_start(rows_of(rows, TT + c), zeros[:]).then_inc(rows_cleared, 16)
            sync.wait_ge(rows_cleared, 32 * (SLOTS // P))
            for u in range(2):
                sync.wait_ge(x1_stored[u], 16 * (TT // 2))
                sync.wait_ge(h2_stored[u], 16 * (TT // 2))

        @block.gpsimd
        def _(pool):
            nc.gpsimd.memset(zeros[:], 0.0).then_inc(zeros_ready, 1)
            nc.gpsimd.memset(empty_slot[:].bitcast(F32), 0.0).then_inc(const_step, 1)
            nc.gpsimd.memset(before[:], 1.0).then_inc(const_step, 1)
            nc.gpsimd.memset(earlier_tok[:], 1.0).then_inc(const_step, 1)
            nc.gpsimd.memset(ones_bf[:], 1.0).then_inc(const_ready, 1)
            nc.gpsimd.iota(expert_iota[:], [[1, EXPERTS]], base=0, channel_multiplier=0,
                           allow_small_or_imprecise_dtypes=True).then_inc(const_ready, 1)
            nc.gpsimd.iota(full_iota[:], [[SLOTS, MOST]], base=0, channel_multiplier=0,
                           allow_small_or_imprecise_dtypes=True).then_inc(const_ready, 1)
            nc.gpsimd.iota(tile_iota[:], [[1, SLOT_TILES]], base=0, channel_multiplier=0,
                           allow_small_or_imprecise_dtypes=True).then_inc(const_ready, 1)
            nc.gpsimd.iota(persist.token_id[:], [[P, TT]], base=0, channel_multiplier=1).then_inc(const_ready, 1)
            pool.wait_ge(const_step, 3)
            nc.gpsimd.iota(empty_slot[:, :, 0], [[1, SLOTS]], base=TOKENS, channel_multiplier=0).then_inc(const_ready, 1)
            nc.gpsimd.affine_select(out=before[:], in_=before[:], compare_op=ALU.is_gt, fill=0.0, base=0,
                                    pattern=[[1, EXPERTS], [-1, EXPERTS]], channel_multiplier=0).then_inc(const_ready, 1)
            nc.gpsimd.affine_select(out=earlier_tok[:], in_=earlier_tok[:], compare_op=ALU.is_gt, fill=0.0, base=0,
                                    pattern=[[1, P]], channel_multiplier=-1).then_inc(const_ready, 1)
            pool.wait_ge(const_ready, 8)
            pool.dma_start(persist.slot_table.rearrange("(c p) o -> c p o", p=SLOTS), empty_slot[:]).then_inc(cleared, 16)
            pool.wait_ge(consts_loaded, 32)

            def modulate(t, u):
                pool.wait_ge(xn_ready, t + 1)
                nc.gpsimd.tensor_tensor(h2[:, u], h2[:, u], mod[:, 2], ALU.mult).then_inc(h2_scaled, 1)
                pool.wait_ge(h2_scaled, t + 1)
                nc.gpsimd.tensor_tensor(h2[:, u], h2[:, u], mod[:, 1], ALU.add).then_inc(h2_ready, 1)

            staged(pool, TT, [(modulate, 2)])

            pool.wait_ge(cleared, 16)

        @block.scalar
        def _(act):
            act.wait_ge(consts_loaded, 32)
            nc.scalar.activation(gate_hi[:], gate_raw[:], ACT.Copy).then_inc(gate_hi_ready, 1)

            def std(t, u):
                act.wait_ge(var_ready, t + 1)
                nc.scalar.activation(small[:, 1:2], small[:, 0:1], ACT.Sqrt).then_inc(std_ready, 1)

            def split_hi(t, u):
                act.wait_ge(h2T_summed, t + 1)
                nc.scalar.activation(h2T_hi[:, :, bass.ds(t * P, P)], ps_t[u][:].rearrange("p (k n) -> p k n", n=P),
                                     ACT.Copy).then_inc(hi_ready, 1)

            def store_h2(t, u):
                act.wait_ge(h2_ready, t + 1)
                act.dma_start(rows_of(persist.h2_dram, t), h2[:, u]).then_inc(h2_stored[u], 16)

            def keep_logits(t, u):
                act.wait_ge(logitsT_summed, t + 1)
                nc.scalar.activation(logitsT[:, bass.ds(t * P, P)], ps_l[u][0:LOGITS, 0:P], ACT.Copy).then_inc(logitsT_ready, 1)

            staged(act, TT, [(std, 2), (store_h2, 1), (split_hi, 1), (keep_logits, 0)])
            act.wait_ge(shifted_ready, 1)
            nc.scalar.activation(exps[:], shifted[:], ACT.Exp).then_inc(exps_ready, 1)
            nc.scalar.activation(gate_exp[:], logits[:, :, EXPERTS], ACT.Exp, scale=-1.0).then_inc(exps_ready, 1)

        @block.vector
        def _(vec):
            vec.wait_ge(gate_hi_ready, 1)
            nc.vector.tensor_tensor(gate_lo[:], gate_raw[:], gate_hi[:].bitcast(F32), ALU.subtract).then_inc(gate_lo_ready, 1)
            NORM_STEPS = 3

            def gate_attention(t, u):
                vec.wait_ge(x_loaded[u], 16 * (t // 2 + 1) if isinstance(t, int) else (t - u) * 8 + 16)
                if not (isinstance(t, int) and t < 2):
                    vec.wait_ge(x1_stored[u], 16 * (t // 2) if isinstance(t, int) else (t - u) * 8)
                    vec.wait_ge(xn_ready, t - 1)
                nc.vector.tensor_tensor(x1[:, u], tile_of(R, t)[:, 0:DIM], mod[:, 0], ALU.mult).then_inc(scaled, 1)

            def add_x(t, u):
                vec.wait_ge(scaled, t + 1)
                nc.vector.tensor_tensor(x1[:, u], x1[:, u], x_in[:, u], ALU.add).then_inc(x1_ready, 1)

            def take_stats(t, u):
                vec.wait_ge(x1_ready, t + 1)
                nc.vector.bn_stats(stats[:], x1[:, u]).then_inc(norm_step, 1)

            def aggregate(t, u):
                vec.wait_ge(norm_step, t * NORM_STEPS + 1)
                settle(vec, persist.settled)
                nc.vector.bn_aggr(mv[:], stats[:]).then_inc(norm_step, 1)

            def add_eps(t, u):
                vec.wait_ge(norm_step, t * NORM_STEPS + 2)
                nc.vector.tensor_scalar(small[:, 0:1], mv[:, 1:2], EPS, None, ALU.add).then_inc(var_ready, 1)

            def normalise(t, u):
                vec.wait_ge(std_ready, t + 1)
                nc.vector.reciprocal(small[:, 2:3], small[:, 1:2]).then_inc(norm_step, 1)
                vec.wait_ge(norm_step, t * NORM_STEPS + 3)
                if not (isinstance(t, int) and t < 2):
                    vec.wait_ge(h2_stored[u], 16 * (t // 2) if isinstance(t, int) else (t - u) * 8)
                nc.vector.tensor_scalar(h2[:, u], x1[:, u], mv[:, 0:1], small[:, 2:3],
                                        ALU.subtract, ALU.mult).then_inc(xn_ready, 1)

            def split_lo(t, u):
                vec.wait_ge(hi_ready, t + 1)
                cols = bass.ds(t * P, P)
                nc.vector.tensor_tensor(h2T_lo[:, :, cols], ps_t[u][:].rearrange("p (k n) -> p k n", n=P),
                                        h2T_hi[:, :, cols].bitcast(F32), ALU.subtract).then_inc(lo_ready, 1)

            staged(vec, TT, [(take_stats, 2), (gate_attention, 3), (aggregate, 2), (add_x, 3), (add_eps, 2),
                             (split_lo, 0), (normalise, 2)], peeled=2)

            steps = [0]

            def then(instruction):
                steps[0] += 1
                instruction.then_inc(route_step, 1)
                vec.wait_ge(route_step, steps[0])

            vec.wait_ge(logits_turned, 1)
            vec.wait_ge(const_ready, 8)
            then(nc.vector.tensor_copy(logits[:], ps_g[:]))
            then(nc.vector.reduce_max(top_logit[:], logits[:, :, 0:EXPERTS], X))
            nc.vector.tensor_tensor(shifted[:], logits[:, :, 0:EXPERTS], top_logit[:].to_broadcast([P, TT, EXPERTS]),
                                    ALU.subtract).then_inc(shifted_ready, 1)
            vec.wait_ge(exps_ready, 2)
            then(nc.vector.tensor_scalar(persist.shared_gate[:], gate_exp[:], 1.0, None, ALU.add))
            then(nc.vector.reciprocal(persist.shared_gate[:], persist.shared_gate[:]))
            then(nc.vector.reduce_sum(exp_sum[:], exps[:], X))
            then(nc.vector.reciprocal(exp_inv[:], exp_sum[:]))
            then(nc.vector.tensor_tensor(routing[:], exps[:], exp_inv[:].to_broadcast([P, TT, EXPERTS]), ALU.mult))
            for t in range(TT):
                last = nc.vector.max(persist.top_weight[:, t], routing[:, t])
            then(last)
            for t in range(TT):
                last = nc.vector.max_index(top_index[:, t], persist.top_weight[:, t], routing[:, t])
            then(last)
            then(nc.vector.tensor_copy(top_number[:], top_index[:, :, 0:TOP]))
            each = [P, TT, TOP, EXPERTS]
            then(nc.vector.tensor_tensor(chosen[:], top_number[:].unsqueeze(3).to_broadcast(each),
                                         expert_iota[:].unsqueeze(1).unsqueeze(1).to_broadcast(each), ALU.is_equal))
            with nc.allow_low_precision(reason="a token picks an expert at most once: 0 or 1"):
                nc.vector.tensor_reduce(member[:], chosen[:].rearrange("p t j e -> p t e j"), axis=X,
                                        op=ALU.add).then_inc(member_ready, 1)
            vec.wait_ge(counted, 1)
            then(nc.vector.tensor_copy(counts[:], ps_count[:]))
            wide = [P, EXPERTS, MOST]
            then(nc.vector.tensor_tensor(above[:], counts[:].to_broadcast(wide), full_iota[:].to_broadcast(wide), ALU.is_gt))
            then(nc.vector.reduce_sum(n_tiles[:, 0], above[:], X))
            then(nc.vector.tensor_tensor(earlier[:], n_tiles[:].to_broadcast([P, EXPERTS, EXPERTS]), before[:], ALU.mult))
            then(nc.vector.reduce_sum(first_tile[:], earlier[:], X))
            then(nc.vector.tensor_tensor(end_tile[:, 0], first_tile[:], n_tiles[:, 0], ALU.add))
            then(nc.vector.tensor_scalar(first_slot[:, 0], first_tile[:], float(SLOTS), None, ALU.mult))
            then(nc.vector.tensor_tensor(slot_of[:], ps_pos[:], first_slot[:].to_broadcast([P, TT, EXPERTS]), ALU.add))
            then(nc.vector.tensor_tensor(picked[:], chosen[:], slot_of[:].unsqueeze(2).to_broadcast(each), ALU.mult))
            then(nc.vector.reduce_sum(slot_number[:], picked[:], X))
            then(nc.vector.tensor_copy(persist.slots[:], slot_number[:]))
            tall = [P, SLOT_TILES, EXPERTS]
            then(nc.vector.tensor_tensor(passed[:], end_tile[:].to_broadcast(tall), tile_iota[:].to_broadcast(tall), ALU.is_le))
            then(nc.vector.reduce_sum(tile_number[:], passed[:], X))
            then(nc.vector.tensor_scalar(tile_number[:], tile_number[:], float(EXPERTS - 1), None, ALU.min))
            then(nc.vector.tensor_copy(persist.tile_expert[:], tile_number[:]))

        @block.tensor
        def _(pe):
            def transpose_h2(t, u):
                pe.wait_ge(h2_ready, t + 1)
                for k in range(KC):
                    last = nc.tensor.transpose(ps_t[u][:, k * P:(k + 1) * P], h2[:, u, k * P:(k + 1) * P], ident[:])
                last.then_inc(h2T_summed, 1)

            def take_logits(t, u):
                pe.wait_ge(lo_ready, t + 1)
                if not (isinstance(t, int) and t < 2):
                    pe.wait_ge(logitsT_ready, t - 1)
                cols = bass.ds(t * P, P)
                for k in range(KC):
                    for m, (a, b) in enumerate(((gate_lo, h2T_hi), (gate_hi, h2T_lo), (gate_hi, h2T_hi))):
                        last = nc.tensor.matmul(ps_l[u][0:LOGITS, 0:P], a[:, k, :], b[:, k, cols],
                                                start=k == 0 and m == 0, stop=k == KC - 1 and m == 2)
                last.then_inc(logitsT_summed, 1)

            pe.wait_ge(gate_lo_ready, 1)
            staged(pe, TT, [(transpose_h2, 1), (take_logits, 0)], peeled=2)
            pe.wait_ge(logitsT_ready, TT)
            for t in range(TT):
                last = nc.tensor.transpose(ps_g[:, t], logitsT[:, t * P:(t + 1) * P], ident[0:LOGITS, 0:LOGITS])
            last.then_inc(logits_turned, 1)
            pe.wait_ge(member_ready, 1)
            nc.tensor.matmul(ps_pos[:], earlier_tok[:], member[:], start=True, stop=False)
            for t in range(TT - 1):
                nc.tensor.matmul(ps_pos[:, t + 1:], ones_bf[:],
                                 member[:, t].unsqueeze(1).to_broadcast([P, TT - 1 - t, EXPERTS]),
                                 start=False, stop=t == TT - 2)
            for t in range(TT):
                last = nc.tensor.matmul(ps_count[:, :, 0], ones_bf[:], member[:, t], start=t == 0, stop=t == TT - 1)
            last.then_inc(counted, 1)



CHUNKS = SHARED // P
PARTS = [(0, P), (P, 2 * P), (2 * P, INNER)]
W13 = KC * 2 * INNER
W2 = len(PARTS) * DIM
TAIL = INNER - 2 * P
SPANS = TOKENS // DIM


def load_expert(sync, persist, w_experts, w_tails, t, u):
    e = sync.value_load(persist.tile_expert[0:1, t:t + 1] if isinstance(t, int) else
                        persist.tile_expert[0:1, bass.ds(t, 1)], min_val=0, max_val=EXPERTS - 1)
    sync.dma_start(persist.ex_raw[u][:, 0:W13 + 2 * DIM],
                   w_experts[bass.ds(e, 1)].rearrange("o p n -> p (o n)")).then_inc(persist.ex_loaded[u], 16)
    sync.dma_start(persist.ex_raw[u][0:TAIL, W13 + 2 * DIM:],
                   w_tails[bass.ds(e, 1)].rearrange("o p n -> p (o n)")).then_inc(persist.ex_loaded[u], 16)


def gather_rows(nc, pool, persist, t, u):
    tokens = persist.slot_tok[:, 2 * t:2 * t + 2] if isinstance(t, int) else persist.slot_tok[:, bass.ds(2 * t, 2)]
    nc.gpsimd.tensor_copy(persist.now[u][:], tokens).then_inc(persist.now_ready, 1)
    pool.wait_ge(persist.now_ready, t + 1)
    settle(pool, persist.settled)
    for c in range(2):
        pool.indirect_dma_start(persist.rows[u][:, c], None, persist.h2_dram,
                                bass.IndirectOffsetOnAxis(ap=persist.now[u][:, c:c + 1], axis=0)
                                ).then_inc(persist.gathered[u], 16)


def shared_expert(nc, persist, w_shared_t, w_experts, w_tails):
    GU = KC * 2 * P
    ctx = ExitStack()
    with ctx:
        def sb(name, shape, dt=F32):
            return ctx.enter_context(nc.sbuf_tensor(name, shape, dt))

        def sem(name):
            return ctx.enter_context(nc.semaphore(name))

        h2T_hi, h2T_lo, total = persist.wide_hi, persist.wide_lo, sb("shared_sum", [P, TT, DIM])
        raw = [sb(f"sh_raw{i}", [P, GU + DIM]) for i in range(2)]
        w_hi = [sb(f"sh_hi{i}", [P, GU + DIM], F32R) for i in range(2)]
        w_lo = [sb(f"sh_lo{i}", [P, GU + DIM], F32R) for i in range(2)]
        silu = [sb(f"sh_silu{i}", [P, DIM]) for i in range(2)]
        act_sb = [sb(f"sh_act{i}", [P, DIM]) for i in range(2)]
        a_hi = [sb(f"sh_a_hi{i}", [P, DIM], F32R) for i in range(2)]
        a_lo = [sb(f"sh_a_lo{i}", [P, DIM], F32R) for i in range(2)]
        ps_gu = [ctx.enter_context(nc.psum_tensor(f"ps_gu{i}", [P, 2, DIM], F32)) for i in range(2)]
        ps_y = [ctx.enter_context(nc.psum_tensor(f"ps_y{i}", [P, DIM], F32)) for i in range(4)]

        slot_rows_f = sb("slot_rows_f", [2 * SLOT_TILES, 2, P])
        put_slot = [sb(f"put_slot{i}", [P, TOP], I32) for i in range(2)]
        entry = [sb(f"entry{i}", [P, TOP, 2], I32) for i in range(2)]

        gate_loaded = sem("gate_b_loaded")
        share_ready = sem("share_ready")
        table_step = sem("table_step")
        table_turned = sem("table_turned")
        table_ready = sem("table_ready")
        share_added = sem("share_added")
        put_copied = sem("put_copied")
        put = [sem(f"put{i}") for i in range(2)]
        loaded = [sem(f"sh_loaded{i}") for i in range(2)]
        w_hi_ready = sem("sh_hi_ready")
        w_lo_ready = sem("sh_lo_ready")
        gu_ready = sem("gu_ready")
        silu_ready = sem("silu_ready")
        act_ready = sem("act_ready")
        a_hi_ready = sem("a_hi_ready")
        a_lo_ready = sem("a_lo_ready")
        y_ready = sem("y_ready")
        y_added = sem("y_added")
        block = ctx.enter_context(nc.Block())
        CREDITS = 4
        N = CHUNKS * SPANS
        PERIOD = 2 * SPANS

        def chunk_of(t, u):
            return t // SPANS if isinstance(t, int) else (t - u % SPANS) // SPANS

        @block.sync
        def _(sync):
            for j in range(2):
                sync.dma_start(raw[j][:], w_shared_t[j]).then_inc(loaded[j], 16)
            sync.dma_start(persist.gate_b[:], persist.mod_dram[:, 3]).then_inc(gate_loaded, 16)

            def load(j, u):
                sync.wait_ge(w_hi_ready, j - 1)
                sync.wait_ge(w_lo_ready, j - 1)
                sync.dma_start(raw[u][:], w_shared_t[bass.ds(j, 1)].rearrange("o p n -> p (o n)")).then_inc(loaded[u], 16)

            with sync.Fori(0, (CHUNKS - 2) // 2) as i:
                for u in (0, 1):
                    load(2 * i + 2 + u, u)
            load(CHUNKS - 1, 0)
            for u in range(2):
                sync.wait_ge(put[u], 16 * TOP * (TT // 2))
            sync.dma_start(persist.slot_rows[:], persist.slot_table.rearrange("(c p) o -> c p o", p=P)).then_inc(persist.table_loaded, 16)
            for u in range(2):
                load_expert(sync, persist, w_experts, w_tails, u, u)

        @block.gpsimd
        def _(pool):
            def enter(t, u):
                if not (isinstance(t, int) and t < 2):
                    pool.wait_ge(put[u], 16 * TOP * (t // 2) if isinstance(t, int) else (t - u) * (8 * TOP))
                nc.gpsimd.tensor_copy(put_slot[u][:], tile_of(persist.slots, t)).then_inc(put_copied, 1)
                number = persist.token_id[:, t:t + 1] if isinstance(t, int) else persist.token_id[:, bass.ds(t, 1)]
                nc.gpsimd.tensor_copy(entry[u][:, :, 0], number.to_broadcast([P, TOP])).then_inc(put_copied, 1)
                nc.gpsimd.tensor_copy(entry[u][:].bitcast(F32)[:, :, 1],
                                      tile_of(persist.top_weight, t)[:, 0:TOP]).then_inc(put_copied, 1)
                pool.wait_ge(put_copied, 3 * t + 3)
                settle(pool, persist.settled)
                for j in range(TOP):
                    pool.indirect_dma_start(persist.slot_table,
                                            bass.IndirectOffsetOnAxis(ap=put_slot[u][:, j:j + 1], axis=0),
                                            entry[u][:, j], None).then_inc(put[u], 16)

            staged(pool, TT, [(enter, 0)], peeled=2)
            for u in range(2):
                pool.wait_ge(put[u], 16 * TOP * (TT // 2))
            for c in range(0, TT, 2):
                if c == TT // 2:
                    pool.wait_ge(table_ready, 2)
                    gather_rows(nc, pool, persist, 0, 0)
                    gather_rows(nc, pool, persist, 1, 1)
                pool.wait_ge(share_ready, c + 2)
                pool.dma_start(rows_of(persist.out, c // 2, 2 * P).rearrange("(c p) n -> p c n", p=P),
                               total[:, c:c + 2], accum_op=ALU.add).then_inc(share_added, 16)
            pool.wait_ge(share_added, 16 * (TT // 2))

        @block.scalar
        def _(act):
            def split_weights(j, u):
                act.wait_ge(loaded[u], 16 * (j // 2 + 1) if isinstance(j, int) else (j - u) * 8 + 16)
                nc.scalar.activation(w_hi[u][:], raw[u][:], ACT.Copy).then_inc(w_hi_ready, 1)

            def hidden(t, u):
                v = u % 2
                if u % SPANS == 1 and not (isinstance(t, int) and t > N - SPANS):
                    j = chunk_of(t, u)
                    if not (isinstance(t, int) and t < SPANS):
                        act.wait_ge(y_ready, (t - u % SPANS) * 4)
                    split_weights(j + 1, (u // SPANS + 1) % 2)
                act.wait_ge(gu_ready, t + 1)
                nc.scalar.activation(silu[v][:], ps_gu[v][:, 0], ACT.Silu).then_inc(silu_ready, 1)
                act.wait_ge(act_ready, t + 1)
                nc.scalar.activation(a_hi[v][:], act_sb[v][:], ACT.Copy).then_inc(a_hi_ready, 1)

            split_weights(0, 0)
            staged(act, N, [(hidden, 0)], PERIOD, peeled=PERIOD)

        @block.vector
        def _(vec):
            def split_weights(j, u):
                vec.wait_ge(w_hi_ready, j + 1)
                nc.vector.tensor_tensor(w_lo[u][:], raw[u][:], w_hi[u][:].bitcast(F32), ALU.subtract).then_inc(w_lo_ready, 1)

            def hidden(t, u):
                v = u % 2
                vec.wait_ge(silu_ready, t + 1)
                nc.vector.tensor_tensor(act_sb[v][:], silu[v][:], ps_gu[v][:, 1], ALU.mult).then_inc(act_ready, 1)
                vec.wait_ge(a_hi_ready, t + 1)
                nc.vector.tensor_tensor(a_lo[v][:], act_sb[v][:], a_hi[v][:].bitcast(F32), ALU.subtract).then_inc(a_lo_ready, 1)
                if u % SPANS == 1 and not (isinstance(t, int) and t > N - SPANS):
                    split_weights(chunk_of(t, u) + 1, (u // SPANS + 1) % 2)
                if isinstance(t, int) and t == N - 2:
                    vec.wait_ge(persist.table_loaded, 16)
                    nc.vector.tensor_copy(slot_rows_f[:, 0], persist.slot_rows[:, :, 0]).then_inc(table_step, 1)
                    nc.vector.tensor_copy(slot_rows_f[:, 1], persist.slot_rows[:].bitcast(F32)[:, :, 1]).then_inc(table_step, 1)
                if isinstance(t, int) and t == N - 1:
                    vec.wait_ge(table_turned, 2)
                    nc.vector.tensor_copy(persist.slot_tok[:], ps_gu[0][:, 0, 0:2 * SLOT_TILES]).then_inc(table_ready, 1)
                    nc.vector.tensor_copy(persist.slot_weight[:], ps_gu[0][:, 1, 0:2 * SLOT_TILES]).then_inc(table_ready, 1)

            def add(t, u):
                for c in range(4):
                    vec.wait_ge(y_ready, 4 * t + (c + 1))
                    row = total[:, (u % SPANS) * 4 + c]
                    if isinstance(t, int) and t < SPANS:
                        nc.vector.tensor_copy(row, ps_y[c][:]).then_inc(y_added, 1)
                    else:
                        nc.vector.tensor_tensor(row, row, ps_y[c][:], ALU.add).then_inc(y_added, 1)
                if isinstance(t, int) and t >= N - SPANS:
                    vec.wait_ge(gate_loaded, 16)
                    vec.wait_ge(y_added, CREDITS + 4 * t + 4)
                    for c in range(4):
                        n = (t % SPANS) * 4 + c
                        nc.vector.scalar_tensor_tensor(total[:, n], total[:, n], persist.shared_gate[:, n:n + 1],
                                                       persist.gate_b[:], ALU.mult, ALU.mult).then_inc(share_ready, 1)

            split_weights(0, 0)
            staged(vec, N, [(hidden, 0), (add, -1)], PERIOD, peeled=SPANS)

        @block.tensor
        def _(pe):
            pe.sem_inc(y_added, CREDITS)

            def up(t, u):
                w, v = (u // SPANS) % 2, u % 2
                if u % SPANS == 0:
                    pe.wait_ge(w_lo_ready, chunk_of(t, u) + 1)
                if not (isinstance(t, int) and t < 2):
                    pe.wait_ge(act_ready, t - 1)
                cols = bass.ds((u % SPANS) * DIM, DIM)
                for half in range(2):
                    for k in range(KC):
                        at = (2 * k + half) * P
                        for m, (a, b) in enumerate(((w_lo, h2T_hi), (w_hi, h2T_lo), (w_hi, h2T_hi))):
                            last = nc.tensor.matmul(ps_gu[v][:, half], a[w][:, at:at + P], b[:, k, cols],
                                                    start=k == 0 and m == 0, stop=k == KC - 1 and m == 2)
                last.then_inc(gu_ready, 1)

            def down(t, u):
                w, v = (u // SPANS) % 2, u % 2
                if isinstance(t, int) and t == N - 2:
                    pe.wait_ge(table_step, 2)
                    pe.wait_ge(act_ready, N - 1)
                    for n in range(2):
                        nc.tensor.transpose(ps_gu[0][:, n, 0:2 * SLOT_TILES], slot_rows_f[:, n],
                                            persist.ident[0:2 * SLOT_TILES, 0:2 * SLOT_TILES]).then_inc(table_turned, 1)
                pe.wait_ge(a_lo_ready, t + 1)
                for c in range(4):
                    rows = slice(c * P, (c + 1) * P)
                    pe.wait_ge(y_added, 4 * t + (c + 1))
                    nc.tensor.matmul(ps_y[c][:], a_lo[v][:, rows], w_hi[w][:, GU:], start=True, stop=False)
                    nc.tensor.matmul(ps_y[c][:], a_hi[v][:, rows], w_lo[w][:, GU:], start=False, stop=False)
                    nc.tensor.matmul(ps_y[c][:], a_hi[v][:, rows], w_hi[w][:, GU:], start=False,
                                     stop=True).then_inc(y_ready, 1)

            staged(pe, N, [(up, 0), (down, -1)], PERIOD, peeled=1)



def routed_experts(nc, persist, w_experts, w_tails):
    ctx = ExitStack()
    with ctx:
        def sb(name, shape, dt=F32):
            return ctx.enter_context(nc.sbuf_tensor(name, shape, dt))

        def sem(name):
            return ctx.enter_context(nc.semaphore(name))

        ident = persist.ident
        raw, rows, slot_tok, slot_weight = persist.ex_raw, persist.rows, persist.slot_tok, persist.slot_weight
        flat_hi = persist.wide_hi[:].rearrange("p k n -> p (k n)")
        flat_lo = persist.wide_lo[:].rearrange("p k n -> p (k n)")
        w13_hi = [flat_hi[:, i * W13:(i + 1) * W13] for i in range(2)]
        w13_lo = [flat_lo[:, i * W13:(i + 1) * W13] for i in range(2)]
        w2_hi = [sb(f"w2_hi{i}", [P, W2], F32R) for i in range(2)]
        w2_lo = [sb(f"w2_lo{i}", [P, W2], F32R) for i in range(2)]
        dest = [sb(f"dest{i}", [P, 2], I32) for i in range(2)]
        xT_hi = [sb(f"xT_hi{i}", [P, KC, SLOTS], F32R) for i in range(2)]
        xT_lo = [sb(f"xT_lo{i}", [P, KC, SLOTS], F32R) for i in range(2)]
        silu = sb("ex_silu", [P, 3, SLOTS])
        hidden = sb("ex_hidden", [P, 3, SLOTS])
        a_hi = [sb(f"ex_a_hi{i}", [P, 3, SLOTS], F32R) for i in range(2)]
        a_lo = [sb(f"ex_a_lo{i}", [P, 3, SLOTS], F32R) for i in range(2)]
        y_sb = [sb(f"y_sb{i}", [P, 2, DIM]) for i in range(2)]
        ps_x = ctx.enter_context(nc.psum_tensor("ex_ps_x", [P, KC, SLOTS], F32))
        ps_gu = [ctx.enter_context(nc.psum_tensor(f"ex_ps_gu{i}", [P, 2, SLOTS], F32)) for i in range(3)]
        ps_y = ctx.enter_context(nc.psum_tensor("ex_ps_y", [P, 2, DIM], F32))

        w_loaded, gathered = persist.ex_loaded, persist.gathered
        x_turned = sem("x_turned")
        x_hi_ready = sem("x_hi_ready")
        x_lo_ready = sem("x_lo_ready")
        w13_hi_ready = sem("w13_hi_ready")
        w13_lo_ready = sem("w13_lo_ready")
        w2_hi_ready = sem("w2_hi_ready")
        w2_lo_ready = sem("w2_lo_ready")
        gu_ready = sem("ex_gu_ready")
        silu_ready = sem("ex_silu_ready")
        hidden_ready = sem("hidden_ready")
        a_hi_ready = sem("ex_a_hi_ready")
        a_lo_ready = sem("ex_a_lo_ready")
        y_ready = sem("ex_y_ready")
        y_taken = sem("y_taken")
        dest_ready = sem("dest_ready")
        added = [sem(f"added{i}") for i in range(2)]
        block = ctx.enter_context(nc.Block())
        N = SLOT_TILES

        def arrivals(t, u, each=16):
            return each * (t // 2 + 1) if isinstance(t, int) else (t - u) * (each // 2) + each

        @block.sync
        def _(sync):
            def load(t, u):
                sync.wait_ge(w2_hi_ready, 2 * t - 2)
                sync.wait_ge(w2_lo_ready, 2 * t - 2)
                load_expert(sync, persist, w_experts, w_tails, t, u)

            staged(sync, N - 2, [(lambda t, u: load(t + 2, u), 0)])

        @block.gpsimd
        def _(pool):
            def gather(t, u):
                if not (isinstance(t, int) and t < 2):
                    pool.wait_ge(x_turned, t - 1)
                    gather_rows(nc, pool, persist, t, u)

            def add(t, u):
                pool.wait_ge(y_taken, 2 * t + 2)
                if not (isinstance(t, int) and t == 0):
                    pool.wait_ge(added[1 - u], 32 * ((t + 1) // 2) if isinstance(t, int) else (t + u) * 16)
                nc.gpsimd.tensor_copy(dest[u][:], slot_tok[:, 2 * t:2 * t + 2] if isinstance(t, int) else
                                      slot_tok[:, bass.ds(2 * t, 2)]).then_inc(dest_ready, 1)
                pool.wait_ge(dest_ready, t + 1)
                settle(pool, persist.settled)
                for c in range(2):
                    pool.indirect_dma_start(persist.out, bass.IndirectOffsetOnAxis(ap=dest[u][:, c:c + 1], axis=0),
                                            y_sb[u][:, c], None, compute_op=ALU.add).then_inc(added[u], 16)

            staged(pool, N, [(gather, 3), (add, -1)], peeled=2)
            for u in range(2):
                pool.wait_ge(added[u], 32 * ((N + 1 - u) // 2))

        @block.scalar
        def _(act):
            def x_hi(t, u):
                act.wait_ge(x_turned, t + 1)
                nc.scalar.activation(xT_hi[u][:], ps_x[:], ACT.Copy).then_inc(x_hi_ready, 1)

            def split_w13(t, u):
                act.wait_ge(w_loaded[u], arrivals(t, u, 32))
                if not (isinstance(t, int) and t < 2):
                    act.wait_ge(gu_ready, 3 * t - 3)
                nc.scalar.activation(w13_hi[u], raw[u][:, 0:W13], ACT.Copy).then_inc(w13_hi_ready, 1)

            def split_w2(t, u):
                if not (isinstance(t, int) and t < 2):
                    act.wait_ge(y_ready, 2 * t - 2)
                nc.scalar.activation(w2_hi[u][:, 0:2 * DIM], raw[u][:, W13:W13 + 2 * DIM],
                                     ACT.Copy).then_inc(w2_hi_ready, 1)
                nc.scalar.activation(w2_hi[u][0:TAIL, 2 * DIM:], raw[u][0:TAIL, W13 + 2 * DIM:],
                                     ACT.Copy).then_inc(w2_hi_ready, 1)

            def activate(t, u):
                for m, (a, b) in enumerate(PARTS):
                    act.wait_ge(gu_ready, 3 * t + (m + 1))
                    nc.scalar.activation(silu[0:b - a, m], ps_gu[m][0:b - a, 0], ACT.Silu).then_inc(silu_ready, 1)
                for m, (a, b) in enumerate(PARTS):
                    act.wait_ge(hidden_ready, 3 * t + (m + 1))
                    nc.scalar.activation(a_hi[u][0:b - a, m], hidden[0:b - a, m], ACT.Copy).then_inc(a_hi_ready, 1)

            staged(act, N, [(x_hi, 1), (split_w13, 1), (activate, 0), (split_w2, 1)], peeled=2)

        @block.vector
        def _(vec):
            def x_lo(t, u):
                vec.wait_ge(x_hi_ready, t + 1)
                nc.vector.tensor_tensor(xT_lo[u][:], ps_x[:], xT_hi[u][:].bitcast(F32), ALU.subtract).then_inc(x_lo_ready, 1)

            def split_w13(t, u):
                vec.wait_ge(w13_hi_ready, t + 1)
                nc.vector.tensor_tensor(w13_lo[u], raw[u][:, 0:W13], w13_hi[u].bitcast(F32),
                                        ALU.subtract).then_inc(w13_lo_ready, 1)

            def split_w2(t, u):
                vec.wait_ge(w2_hi_ready, 2 * t + 2)
                nc.vector.tensor_tensor(w2_lo[u][:, 0:2 * DIM], raw[u][:, W13:W13 + 2 * DIM],
                                        w2_hi[u][:, 0:2 * DIM].bitcast(F32), ALU.subtract).then_inc(w2_lo_ready, 1)
                nc.vector.tensor_tensor(w2_lo[u][0:TAIL, 2 * DIM:], raw[u][0:TAIL, W13 + 2 * DIM:],
                                        w2_hi[u][0:TAIL, 2 * DIM:].bitcast(F32), ALU.subtract).then_inc(w2_lo_ready, 1)

            def multiply(t, u):
                vec.wait_ge(a_lo_ready, 3 * t)
                for m, (a, b) in enumerate(PARTS):
                    vec.wait_ge(silu_ready, 3 * t + (m + 1))
                    nc.vector.tensor_tensor(hidden[0:b - a, m], silu[0:b - a, m], ps_gu[m][0:b - a, 1],
                                            ALU.mult).then_inc(hidden_ready, 1)
                for m, (a, b) in enumerate(PARTS):
                    vec.wait_ge(a_hi_ready, 3 * t + (m + 1))
                    nc.vector.tensor_tensor(a_lo[u][0:b - a, m], hidden[0:b - a, m], a_hi[u][0:b - a, m].bitcast(F32),
                                            ALU.subtract).then_inc(a_lo_ready, 1)

            def weigh(t, u):
                if not (isinstance(t, int) and t < 2):
                    vec.wait_ge(added[u], 32 * (t // 2) if isinstance(t, int) else (t - u) * 16)
                for c in range(2):
                    vec.wait_ge(y_ready, 2 * t + (c + 1))
                    weight = slot_weight[:, 2 * t + c:2 * t + c + 1] if isinstance(t, int) else slot_weight[:, bass.ds(2 * t + c, 1)]
                    nc.vector.scalar_tensor_tensor(y_sb[u][:, c], ps_y[:, c], weight, persist.gate_b[:],
                                                   ALU.mult, ALU.mult).then_inc(y_taken, 1)

            staged(vec, N, [(x_lo, 1), (split_w13, 1), (multiply, 0), (split_w2, 1), (weigh, -1)], peeled=2)

        @block.tensor
        def _(pe):
            def turn(t, u):
                pe.wait_ge(gathered[u], arrivals(t, u, 32))
                pe.wait_ge(x_lo_ready, t)
                for c in range(2):
                    for k in range(KC):
                        last = nc.tensor.transpose(ps_x[:, k, c * P:(c + 1) * P], rows[u][:, c, k * P:(k + 1) * P], ident[:])
                last.then_inc(x_turned, 1)

            def up(t, u):
                pe.wait_ge(x_lo_ready, t + 1)
                pe.wait_ge(w13_lo_ready, t + 1)
                for m, (a, b) in enumerate(PARTS):
                    if not (isinstance(t, int) and t == 0):
                        pe.wait_ge(hidden_ready, 3 * t + (m - 2))
                    for half in range(2):
                        for k in range(KC):
                            at = (2 * k + half) * INNER
                            for n, (w, x) in enumerate(((w13_lo, xT_hi), (w13_hi, xT_lo), (w13_hi, xT_hi))):
                                last = nc.tensor.matmul(ps_gu[m][0:b - a, half], w[u][:, at + a:at + b], x[u][:, k],
                                                        start=k == 0 and n == 0, stop=k == KC - 1 and n == 2)
                    last.then_inc(gu_ready, 1)

            def down(t, u):
                pe.wait_ge(a_lo_ready, 3 * t + 3)
                pe.wait_ge(w2_lo_ready, 2 * t + 2)
                for c in range(2):
                    if not (isinstance(t, int) and t == 0):
                        pe.wait_ge(y_taken, 2 * t + (c - 1))
                    for m, (a, b) in enumerate(PARTS):
                        at = slice(m * DIM, (m + 1) * DIM)
                        cols = slice(c * P, (c + 1) * P)
                        for n, (h, w) in enumerate(((a_lo, w2_hi), (a_hi, w2_lo), (a_hi, w2_hi))):
                            last = nc.tensor.matmul(ps_y[:, c], h[u][0:b - a, m, cols], w[u][0:b - a, at],
                                                    start=m == 0 and n == 0, stop=m == 2 and n == 2)
                    last.then_inc(y_ready, 1)

            staged(pe, N, [(turn, 1), (up, 0), (down, -1)], peeled=1)



class Kept:
    pass


def adaln_block(nc, x, w_qkv_t, b_qkv, rope, c, w_mod_t, gates_t, w_shared_t, w_experts, w_tails, out):
    def kept(name, shape, dt=F32):
        return nc.dram_tensor(name, shape, dt, kind="Internal").ap()

    persist = Kept()
    persist.mod_dram = kept("mod_dram", [P, 4, DIM])
    persist.out = out
    persist.h2_dram = kept("h2_dram", [TOKENS + SLOTS, DIM])
    persist.slot_table = kept("slot_table", [SLOT_TILES * SLOTS, 2], I32)
    with ExitStack() as whole:
        persist.table_loaded = whole.enter_context(nc.semaphore("table_loaded"))
        persist.ex_loaded = [whole.enter_context(nc.semaphore(f"ex_loaded{i}")) for i in range(2)]
        persist.now_ready = whole.enter_context(nc.semaphore("now_ready"))
        persist.gathered = [whole.enter_context(nc.semaphore(f"gathered{i}")) for i in range(2)]
        persist.settled = whole.enter_context(nc.semaphore("settled"))

        def sb(stack, name, shape, dt=F32):
            return stack.enter_context(nc.sbuf_tensor(name, shape, dt))

        persist.wide_hi = sb(whole, "wide_hi", [P, KC, TOKENS], F32R)
        persist.wide_lo = sb(whole, "wide_lo", [P, KC, TOKENS], F32R)
        persist.ident = sb(whole, "ident", [P, P])
        persist.ident_bf = sb(whole, "ident_bf", [P, P], BF16)
        persist.mask = sb(whole, "mask", [P, P], BF16)
        persist.own_tile = sb(whole, "own_tile", [32, TT], BF16)
        persist.top_weight = sb(whole, "top_weight", [P, TT, 8])
        persist.slots = sb(whole, "slots", [P, TT, TOP], I32)
        persist.token_id = sb(whole, "token_id", [P, TT], I32)
        persist.shared_gate = sb(whole, "shared_gate", [P, TT])
        persist.tile_expert = sb(whole, "tile_expert", [P, SLOT_TILES], I32)
        with ExitStack() as attending:
            persist.R = sb(attending, "R", [P, TT, 2 * DIM])
            with ExitStack() as values:
                persist.V = sb(values, "V", [P, TT, HEADS, HEAD + 1])
                norm_and_project(nc, persist, x, w_qkv_t, b_qkv, rope, c, w_mod_t)
                attention(nc, persist)
            norm_and_route(nc, persist, x, gates_t)
        persist.gate_b = sb(whole, "gate_b", [P, DIM])
        persist.ex_raw = [sb(whole, f"ex_raw{i}", [P, W13 + W2]) for i in range(2)]
        persist.slot_tok = sb(whole, "slot_tok", [P, 2 * SLOT_TILES], I32)
        persist.slot_weight = sb(whole, "slot_weight", [P, 2 * SLOT_TILES])
        persist.now = [sb(whole, f"now{i}", [P, 2], I32) for i in range(2)]
        persist.rows = [sb(whole, f"rows{i}", [P, 2, DIM]) for i in range(2)]
        persist.slot_rows = sb(whole, "slot_rows", [2 * SLOT_TILES, P, 2], I32)
        shared_expert(nc, persist, w_shared_t, w_experts, w_tails)
        routed_experts(nc, persist, w_experts, w_tails)


def rope_table():
    inv = (1.0 / np.float32(10000.0) ** (np.arange(0, HEAD, 2, dtype=np.float32) / np.float32(HEAD))).astype(np.float32)
    angle = np.arange(TOKENS, dtype=np.float32)[:, None] * inv[None, :]
    cos, sin = np.cos(angle), np.sin(angle)
    table = np.stack([np.concatenate([cos, cos], 1), np.concatenate([-sin, sin], 1)], 1)
    return np.ascontiguousarray(table.reshape(TT, P, 2, HEAD).transpose(1, 0, 2, 3).astype(np.float32))


def chunked(w):
    return np.ascontiguousarray(w.T.reshape(-1, P, w.shape[0]).transpose(1, 0, 2))


def layout(i):
    a = {}
    a['x'] = i['L0_attn_hidden_states'].reshape(TOKENS, DIM)
    w = i['L0_attn_w_qkv'].reshape(HEADS, 3, HEAD, DIM).transpose(1, 0, 2, 3).reshape(3 * DIM, DIM)
    a['w_qkv_t'] = chunked(w)
    a['b_qkv'] = i['L0_attn_b_qkv'].reshape(HEADS, 3, HEAD).transpose(1, 0, 2).reshape(3 * DIM)
    a['rope'] = rope_table()
    a['c'] = i['L0_c'].reshape(KC, P).T
    a['w_mod_t'] = i['L0_wmod'].reshape(KC, P, 6, DIM).transpose(1, 2, 0, 3)
    a['gates_t'] = chunked(np.concatenate([i['L0_ffn_gate_w'], i['L0_ffn_sgate_w']]))
    gu = i['L0_ffn_shared_gate_up_w'].reshape(2, SHARED // P, P, KC, P)
    gu = gu.transpose(1, 4, 3, 0, 2).reshape(SHARED // P, P, KC * 2 * P)
    down = i['L0_ffn_shared_down_w'].T.reshape(SHARED // P, P, DIM)
    a['w_shared_t'] = np.concatenate([gu, down], 2)
    w13 = i['L0_ffn_w13'].reshape(EXPERTS, 2, INNER, KC, P).transpose(0, 4, 3, 1, 2).reshape(EXPERTS, P, W13)
    w2 = i['L0_ffn_w2'].transpose(0, 2, 1)
    w2_wide = w2[:, :2 * P].reshape(EXPERTS, 2, P, DIM).transpose(0, 2, 1, 3).reshape(EXPERTS, P, 2 * DIM)
    a['w_experts'] = np.concatenate([w13, w2_wide], 2)
    a['w_tails'] = w2[:, 2 * P:]
    return a


_INS = ['x', 'w_qkv_t', 'b_qkv', 'rope', 'c', 'w_mod_t', 'gates_t', 'w_shared_t', 'w_experts', 'w_tails']


def kernel(**inputs):
    import concourse.bacc as _bacc
    from concourse.bass_utils import run_bass_kernel_spmd as _run

    nc = _bacc.Bacc("TRN2", target_bir_lowering=False, num_devices=1)
    laid = layout({name: np.asarray(a) for name, a in inputs.items()})
    arrays, args = {}, []
    for name in _INS:
        a = np.ascontiguousarray(laid[name])
        arrays[f"in_{name}"] = a
        args.append(nc.dram_tensor(f"in_{name}", a.shape, mybir.dt.from_np(a.dtype), kind="ExternalInput").ap())
    out = nc.dram_tensor("out", [TOKENS + SLOTS, DIM], F32, kind="ExternalOutput").ap()
    adaln_block(nc, *args, out)
    r = _run(nc, [arrays], core_ids=[0])
    return r.results[0]["out"][:TOKENS].reshape(1, TOKENS, DIM)
```
